# Optimizing a Trainium2 kernel written in Bass

```python
import numpy as np
import jax
import jax.numpy as jnp

def _softmax(x, axis=-1):
    return jax.nn.softmax(x, axis=axis)

def _gelu(x):
    return jax.nn.gelu(x, approximate=True)

def _silu(x):
    return jax.nn.silu(x)

def _sigmoid(x):
    return jax.nn.sigmoid(x)

def _layernorm(x, axis=-1, eps=1e-05):
    m = jnp.mean(x, axis=axis, keepdims=True)
    v = jnp.var(x, axis=axis, keepdims=True)
    return (x - m) / jnp.sqrt(v + eps)

def _scatter_add(tgt, idx, src, axis=0):
    return tgt.at[idx].add(src)

def _segment_sum(src, seg, n):
    return jax.ops.segment_sum(src, seg, n)
kernel_name = 'mk_conv_attn_hybrid_d2_conv_nchw128_r4_6133c3'

def setup_inputs(seed: int=0):
    np.random.seed(seed)
    _w = jnp.asarray

    def _rec_inputs():
        import jax
        import jax.numpy as jnp
        _gk = jax.random.key(seed)
        x = -0.0002023 + 1 * jax.random.normal(jax.random.fold_in(_gk, 1), (16, 32, 56, 56), jnp.float32)
        return x
    x = _rec_inputs()

    def _L0_conv_setup():
        import math
        import jax, jax.numpy as jnp
        import numpy as np
        from jax import lax
        N, C, H, W = (16, 32, 56, 56)

        def _conv(x, w, padding, dilation=(1, 1), groups=1):
            return lax.conv_general_dilated(x, w, window_strides=(1, 1), padding=[(padding[0], padding[0]), (padding[1], padding[1])], rhs_dilation=dilation, dimension_numbers=('NCHW', 'OIHW', 'NCHW'), feature_group_count=groups)
        key = jax.random.key(seed)
        ks = jax.random.split(key, 6)
        x = jax.random.normal(ks[0], (N, C, H, W), jnp.float32)
        w2 = jax.random.normal(ks[1], (C, C, 1, 3), jnp.float32) * 0.05
        p6w = jax.random.normal(ks[2], (1, C, 7, 1), jnp.float32) * 0.02
        w7 = jax.random.normal(ks[3], (C, 1, 1, 5), jnp.float32) * 0.05
        w8 = jax.random.normal(ks[4], (C, 1, 5, 5), jnp.float32) * 0.05
        p9w = jax.random.normal(ks[5], (1, 1, 7, C), jnp.float32) * 0.02
        return {'x': x, 'w2': w2, 'p6w': p6w, 'w7': w7, 'w8': w8, 'p9w': p9w}
    _L0_conv_all = _L0_conv_setup()
    _L0_conv_in = {k: v for k, v in _L0_conv_all.items() if k in ('w2', 'p6w', 'w7', 'w8', 'p9w')}
    del _L0_conv_all

    def _L1_attn_setup():
        import jax, jax.numpy as jnp
        import numpy as np
        B, S, D = (4, 1024, 32)
        key = jax.random.key(seed)
        ks = jax.random.split(key, 4)
        scale = 1.0 / np.sqrt(D)
        return {'x': jax.random.normal(ks[0], (B, S, D), dtype=jnp.float32), 'Wq': jax.random.normal(ks[1], (D, D), dtype=jnp.float32) * scale, 'bq': jnp.zeros((D,), dtype=jnp.float32), 'Wk': jax.random.normal(ks[2], (D, D), dtype=jnp.float32) * scale, 'bk': jnp.zeros((D,), dtype=jnp.float32), 'Wv': jax.random.normal(ks[3], (D, D), dtype=jnp.float32) * scale, 'bv': jnp.zeros((D,), dtype=jnp.float32)}
    _L1_attn_all = _L1_attn_setup()
    _L1_attn_in = {k: v for k, v in _L1_attn_all.items() if k in ('Wq', 'bq', 'Wk', 'bk', 'Wv', 'bv')}
    del _L1_attn_all

    def _L1_ffn_setup():
        import jax, jax.numpy as jnp
        import numpy as np
        B, N, D, C, E, K = (8, 2048, 32, 32, 8, 2)
        key = jax.random.key(seed)
        k0, k1, k2 = jax.random.split(key, 3)
        x = jax.random.normal(k0, (B, N, D), dtype=jnp.float32)
        router_w = jax.random.normal(k1, (D, E), dtype=jnp.float32) * 0.05
        router_b = jnp.zeros((E,), dtype=jnp.float32)
        expert_w = jax.random.normal(k2, (E, D, C), dtype=jnp.float32) * (1.0 / np.sqrt(D))
        expert_b = jnp.zeros((E, C), dtype=jnp.float32)
        return {'x': x, 'router_w': router_w, 'router_b': router_b, 'expert_w': expert_w, 'expert_b': expert_b}
    _L1_ffn_all = _L1_ffn_setup()
    _L1_ffn_in = {k: v for k, v in _L1_ffn_all.items() if k in ('router_w', 'router_b', 'expert_w', 'expert_b')}
    del _L1_ffn_all
    return {'x': x, 'L0_conv_w2': _L0_conv_in['w2'], 'L0_conv_p6w': _L0_conv_in['p6w'], 'L0_conv_w7': _L0_conv_in['w7'], 'L0_conv_w8': _L0_conv_in['w8'], 'L0_conv_p9w': _L0_conv_in['p9w'], 'L1_attn_Wq': _L1_attn_in['Wq'], 'L1_attn_bq': _L1_attn_in['bq'], 'L1_attn_Wk': _L1_attn_in['Wk'], 'L1_attn_bk': _L1_attn_in['bk'], 'L1_attn_Wv': _L1_attn_in['Wv'], 'L1_attn_bv': _L1_attn_in['bv'], 'L1_ffn_router_w': _L1_ffn_in['router_w'], 'L1_ffn_router_b': _L1_ffn_in['router_b'], 'L1_ffn_expert_w': _L1_ffn_in['expert_w'], 'L1_ffn_expert_b': _L1_ffn_in['expert_b']}

def reference(x, L0_conv_w2, L0_conv_p6w, L0_conv_w7, L0_conv_w8, L0_conv_p9w, L1_attn_Wq, L1_attn_bq, L1_attn_Wk, L1_attn_bk, L1_attn_Wv, L1_attn_bv, L1_ffn_router_w, L1_ffn_router_b, L1_ffn_expert_w, L1_ffn_expert_b):
    import jax
    import jax.numpy as jnp

    def _L0_conv_ref(x, w2, p6w, w7, w8, p9w):
        import math
        import jax, jax.numpy as jnp
        import numpy as np
        from jax import lax
        N, C, H, W = (16, 32, 56, 56)

        def _conv(x, w, padding, dilation=(1, 1), groups=1):
            return lax.conv_general_dilated(x, w, window_strides=(1, 1), padding=[(padding[0], padding[0]), (padding[1], padding[1])], rhs_dilation=dilation, dimension_numbers=('NCHW', 'OIHW', 'NCHW'), feature_group_count=groups)
        n, c, h, w = x.shape
        xp = jnp.pad(x, ((0, 0), (0, 0), (0, 0), (6, 6)))
        t1 = jnp.stack([xp[..., 2 * k:2 * k + w] for k in range(7)], axis=2)
        t2 = _conv(x, w2, (0, 1))
        t3 = jnp.einsum('nakhw,nbhw->nakb', t1, x) / math.sqrt(h * w)
        t2p = jnp.pad(t2, ((0, 0), (0, 0), (3, 3), (0, 0)))
        t4 = jnp.stack([t2p[:, :, k:k + h, :] for k in range(7)], axis=2)
        t6 = p6w * t3
        t7 = _conv(t2, w7, (0, 2), groups=c)
        t8 = _conv(x, w8, (4, 4), dilation=(2, 2), groups=c)
        t9 = p9w * t6
        t10 = jnp.einsum('nakb,nakhw->nbhw', t9, t4) / math.sqrt(c * 7)
        t11 = t10 - t7
        t12 = t8 - t11
        return t12

    def _L1_attn_ref(x, Wq, bq, Wk, bk, Wv, bv):
        import jax, jax.numpy as jnp
        import numpy as np
        B, S, D = (4, 1024, 32)
        q = jnp.einsum('bsd,de->bse', x, Wq) + bq
        k = jnp.einsum('bsd,de->bse', x, Wk) + bk
        v = jnp.einsum('bsd,de->bse', x, Wv) + bv
        d = x.shape[-1]
        scores = jnp.einsum('bqd,bkd->bqk', q, k) / jnp.sqrt(jnp.asarray(d, x.dtype))
        attn = jax.nn.softmax(scores, axis=-1)
        out = jnp.einsum('bqk,bkd->bqd', attn, v)
        return out + x

    def _L1_ffn_ref(x, router_w, router_b, expert_w, expert_b):
        import jax, jax.numpy as jnp
        import numpy as np
        B, N, D, C, E, K = (8, 2048, 32, 32, 8, 2)
        router_probs = jax.nn.softmax(x @ router_w + router_b, axis=-1)
        top_p, top_i = jax.lax.top_k(router_probs, K)
        top_p = top_p / jnp.sum(top_p, axis=-1, keepdims=True)
        expert_out = jnp.einsum('bnd,edc->bnec', x, expert_w) + expert_b
        gathered = jnp.take_along_axis(expert_out, top_i[..., None], axis=2)
        return jnp.einsum('bnk,bnkc->bnc', top_p, gathered)

    def _gn(v, G=32, eps=1e-05):
        B_, C_, H_, W_ = v.shape
        g = v.reshape(B_, G, C_ // G, H_, W_)
        m = jnp.mean(g, axis=(2, 3, 4), keepdims=True)
        s = jnp.var(g, axis=(2, 3, 4), keepdims=True)
        return ((g - m) / jnp.sqrt(s + eps)).reshape(v.shape)

    def _ln_c(v, eps=1e-06):
        m = jnp.mean(v, axis=1, keepdims=True)
        s = jnp.var(v, axis=1, keepdims=True)
        return (v - m) / jnp.sqrt(s + eps)

    def _ln_t(v, eps=1e-05):
        m = jnp.mean(v, axis=-1, keepdims=True)
        s = jnp.var(v, axis=-1, keepdims=True)
        return (v - m) / jnp.sqrt(s + eps)

    def _to_tokens(v):
        B_, C_, H_, W_ = v.shape
        return v.reshape(B_, C_, H_ * W_).transpose(0, 2, 1)

    def _from_tokens(t, like):
        B_, C_, H_, W_ = like.shape
        return t.transpose(0, 2, 1).reshape(B_, C_, H_, W_)
    x = x + _L0_conv_ref(_gn(x), L0_conv_w2, L0_conv_p6w, L0_conv_w7, L0_conv_w8, L0_conv_p9w)
    t = _to_tokens(x)
    t = t + _L1_attn_ref(_ln_t(t), L1_attn_Wq, L1_attn_bq, L1_attn_Wk, L1_attn_bk, L1_attn_Wv, L1_attn_bv)
    t = t + _L1_ffn_ref(_ln_t(t), L1_ffn_router_w, L1_ffn_router_b, L1_ffn_expert_w, L1_ffn_expert_b)
    x = _from_tokens(t, x)
    return x

_drawn_inputs = setup_inputs


def setup_inputs(seed=0):
    import zlib

    import numpy as np

    out = dict(_drawn_inputs(seed))
    spreads = {'L1_attn_bq': (0.0, 0.28),
     'L1_attn_bk': (0.0, 0.8),
     'L1_attn_bv': (0.0, 0.1),
     'L1_ffn_router_b': (0.0, 0.1),
     'L1_ffn_expert_b': (0.0, 0.1)}
    factors = {'L0_conv_p6w': 7.461, 'L0_conv_p9w': 8.0}
    for name, (base, spread) in spreads.items():
        noise = np.random.default_rng([zlib.crc32(name.encode()), seed]).standard_normal(out[name].shape)
        drawn = base * np.exp(spread * noise) if base else spread * noise
        out[name] = jnp.asarray(drawn.astype(out[name].dtype))
    for name, factor in factors.items():
        out[name] = (out[name] * factor).astype(out[name].dtype)
    return out
```

```python
import math
from contextlib import ExitStack

import numpy as np
import concourse.bass as bass
from concourse import mybir

F32 = mybir.dt.float32
F16 = mybir.dt.float16
ALU = mybir.AluOpType
ACT = mybir.ActivationFunctionType
AX = mybir.AxisListType

N, C, H, W = 16, 32, 56, 56
P = 128
G = P // C
NG = N // G
T = H * W
TILE = 448
NT = T // TILE
TR = TILE // W
NC = -(-T // P)
LAST = T - (NC - 1) * P
NP = NC // 2
E = 8
GN_EPS, LN_EPS = 1e-5, 1e-5

XW, XTOP, XLEFT = W + 6, 4, 6
XLEN = (H + 2 * XTOP) * XW + 12
XS_LEN = XLEN - 2 * (G - 1)
YW, YTOP, YLEFT = W + 4, 3, 2
YLEN = (H + 2 * YTOP) * YW + 8
YS_LEN = (H + YTOP) * YW + 4
GR = 2 * XW
NGR = H // 2
ORDER_F = 41
ORDER = 33


def newton_rsqrt(link, eng, r, v, t):
    link(eng.tensor_tensor(t, r, r, ALU.mult))
    link(eng.tensor_tensor(t, t, v, ALU.mult))
    link(eng.tensor_scalar(t, t, -0.5, 1.5, ALU.mult, ALU.add))
    return link(eng.tensor_tensor(r, r, t, ALU.mult))


def build_program(nc, x, wts, out):
    def scratch(name, shape, dt):
        return nc.dram_tensor(name, shape, dt, kind="Internal").ap()

    scr = {
        "res": scratch("residual", (N, P, NC * C), F32),
        "val": scratch("values", (N, P, NC * C), F32),
        "ks": scratch("key_stacks", (N, P, T), F16),
        "us": scratch("query_stacks", (N, P, T), F16),
        "sums": scratch("sums", (N, P, T), F32),
        "ident": wts["ident"],
    }
    prepare(nc, x, wts, scr)
    attend(nc, scr)
    finish(nc, wts, scr, out)


def prepare(nc, x, wts, scr):
    with ExitStack() as ctx:
        def sb(name, shape, dt=F32):
            return ctx.enter_context(nc.sbuf_tensor("sb_" + name, shape, dt))

        def ps(name, shape, dt=F32):
            return ctx.enter_context(nc.psum_tensor(name, shape, dt))

        def sem(name):
            return ctx.enter_context(nc.semaphore(name))

        ident = sb("ident", [P, P])
        ident16 = sb("ident16", [P, P], F16)
        eye4 = sb("eye4", [P, C])
        w8s = sb("w8s", [P, 5])
        w8e = sb("w8e", [P, 5])
        w7e = sb("w7e", [P, 5])
        p6 = sb("p6", [P, 2])
        p9 = sb("p9", [P, 2, C])
        lhs8 = sb("lhs8", [P, 5, C])
        lhs2 = sb("lhs2", [P, 2, C])
        p69 = sb("p69", [P, 2, C])
        wqk = sb("wqk", [C, 2, C])
        wqk0 = sb("wqk0", [C, 2, C])
        wqkT = sb("wqkT", [C, 2, C])
        wqkT4 = sb("wqkT4", [C, 2, G, C])
        mfull = sb("mfull", [P, P])
        mstack = sb("mstack", [P, P], F16)
        X1 = sb("X1", [P, NC * P])
        Xp = sb("Xp", [P, XLEN])
        T2 = sb("T2", [P, YLEN])
        TT = sb("TT", [P, 2, NGR, P])
        stacks = sb("stacks", [P, G * XS_LEN])
        XS = stacks[:].rearrange("p (n l) -> p n l", n=G)
        NY = G * NC * P // 2
        Y16 = stacks[:, 0:NY].bitcast(F16).rearrange("p (n k s c) -> p n k s c", n=G, k=NC, s=G)
        KS = stacks[:, NY:NY + T].bitcast(F16).rearrange("p (b t) -> p b t", b=2)
        US = stacks[:, NY + T:NY + 2 * T].bitcast(F16).rearrange("p (b t) -> p b t", b=2)
        stacks2 = sb("stacks2", [P, G * YS_LEN])
        T2S = stacks2[:].rearrange("p (n l) -> p n l", n=G)
        NTM = G * NC * C
        TMf, XHf, SQf = (stacks2[:, i * NTM:(i + 1) * NTM] for i in range(3))
        TM, XH, SQ = (v.rearrange("p (m c) -> p m c", c=C) for v in (TMf, XHf, SQf))
        stats = sb("stats", [P, NT, 6])
        mv = sb("mv", [P, 2])
        var, rs, tmp1 = sb("var", [P, 1]), sb("rs", [P, 1]), sb("tmp1", [P, 1])
        gsb, gT, gB = sb("gsb", [P, G, C]), sb("gT", [P, G, C]), sb("gB", [P, G, C])
        lhs10 = sb("lhs10", [P, 2, G, C])
        M = G * NC
        lsum, lvar, lrs, ltmp = (sb(n, [P, M]) for n in ("lsum", "lvar", "lrs", "ltmp"))

        psA = ps("psA", [P, 2, 512])
        psT = ps("psT", [P, 2, 512])
        psG = ps("psG", [P, 512])
        psK = ps("psK", [P, 2, 1024], F16)

        names = ("w_in w_zero w_dve w_pe x_in xp_ready xs_in stat_var stat_std a_full t2_ready t2s_in t_full "
                 "t_free gram_done lhs10_ready x1_ready tm_cen tm_sq tm_var tm_std xh_ready res_ready scr_out "
                 "val_ready y16_ready k_full ks_ready ks_out0 ks_out1 u_hi u_ready us_out0 us_out1 order")
        (w_in, w_zero, w_dve, w_pe, x_in, xp_ready, xs_in, stat_var, stat_std, a_full, t2_ready, t2s_in, t_full,
         t_free, gram_done, lhs10_ready, x1_ready, tm_cen, tm_sq, tm_var, tm_std, xh_ready, res_ready, scr_out,
         val_ready, y16_ready, k_full, ks_ready, ks_out0, ks_out1, u_hi, u_ready, us_out0, us_out1, order) = map(sem, names.split())
        ks_out, us_out = (ks_out0, ks_out1), (us_out0, us_out1)
        block = ctx.enter_context(nc.Block())

        x_g = x.rearrange("(g n) c h w -> g (n c) (h w)", n=G)
        res_g = scr["res"].rearrange("(g n) p f -> g p n f", n=G)
        val_g = scr["val"].rearrange("(g n) p f -> g p n f", n=G)
        ks_i = scr["ks"].rearrange("(g n) p t -> g n p t", n=G)
        us_i = scr["us"].rearrange("(g n) p t -> g n p t", n=G)
        NW = 14
        KSETS = 4
        TSETS = G * NT + NT
        STEPS = 0

        def xrows(ap, row, col, rows=TR):
            a = row * XW + col
            return ap[..., a:a + rows * XW].rearrange("p (r w) -> p r w", w=XW)[:, :, 0:W]

        def yrows(ap, row, col, rows=TR):
            a = row * YW + col
            return ap[..., a:a + rows * YW].rearrange("p (r w) -> p r w", w=YW)[:, :, 0:W]

        @block.sync
        def _(sp):
            for dst, name in ((ident, "ident"), (ident16, "ident16"), (eye4, "eye4"), (w8s, "w8s"), (w8e, "w8e"),
                              (w7e, "w7e")):
                sp.dma_start(dst[:], wts[name]).then_inc(w_in, 16)
            sp.dma_start(p6[:], wts["p6"]).then_inc(w_in, 16)
            sp.dma_start(p9[:].rearrange("p a c -> p (a c)"), wts["p9"]).then_inc(w_in, 16)
            sp.wait_ge(w_zero, 1)
            sp.dma_start(lhs2[0:C, 0, :], wts["w2t"][0]).then_inc(w_in, 16)
            sp.dma_start(lhs2[C:2 * C, 0, :], wts["w2t"][2]).then_inc(w_in, 16)
            sp.dma_start(lhs2[0:C, 1, :], wts["w2t"][1]).then_inc(w_in, 16)
            sp.dma_start(wqk[1:C, :, :], wts["wqk"][1:C, :].rearrange("p (a c) -> p a c", a=2)).then_inc(w_in, 16)
            sp.dma_start(wqk[0:1, :, :], wts["bqk"].rearrange("p (a c) -> p a c", a=2)).then_inc(w_in, 16)
            sp.dma_start(wqk0[1:C, :, :], wts["wqk"][0:1, :].broadcast_to([C - 1, 2 * C]).rearrange(
                "p (a c) -> p a c", a=2)).then_inc(w_in, 16)
            with sp.Fori(0, NG) as g:
                sp.wait_ge(scr_out, g * 32)
                for b in range(2):
                    sp.wait_ge(ks_out[b], g * 32)
                    sp.wait_ge(us_out[b], g * 32)
                sp.dma_start(X1[:, 0:T], x_g[bass.ds(g, 1)].rearrange("a p t -> (a p) t")).then_inc(x_in, 16)
                sp.wait_ge(xp_ready, g + 1)
                for n in range(G):
                    for s in range(G):
                        sp.dma_start(XS[C * s:C * s + C, n, :],
                                     Xp[C * n:C * n + C, 2 * s:2 * s + XS_LEN]).then_inc(xs_in, 16)
                sp.wait_ge(t2_ready, NT * (g + 1))
                for n in range(G):
                    for s in range(G):
                        sp.dma_start(T2S[C * s:C * s + C, n, :],
                                     T2[C * n:C * n + C, YW * s:YW * s + YS_LEN]).then_inc(t2s_in, 16)
                sp.wait_ge(res_ready, g + 1)
                sp.dma_start(res_g[bass.ds(g, 1)].rearrange("a p n f -> (a p) n f"),
                             TMf.rearrange("p (n f) -> p n f", n=G)).then_inc(scr_out, 16)
                sp.wait_ge(val_ready, g + 1)
                sp.dma_start(val_g[bass.ds(g, 1)].rearrange("a p n f -> (a p) n f"),
                             XHf.rearrange("p (n f) -> p n f", n=G)).then_inc(scr_out, 16)
                for n in range(G):
                    sp.wait_ge(ks_ready, (g * G + n + 1) * KSETS)
                    sp.dma_start(ks_i[bass.ds(g, 1), n].rearrange("a p t -> (a p) t"), KS[:, n % 2]).then_inc(ks_out[n % 2], 16)
                    sp.wait_ge(u_ready, (g * G + n + 1) * NT)
                    sp.dma_start(us_i[bass.ds(g, 1), n].rearrange("a p t -> (a p) t"), US[:, n % 2]).then_inc(us_out[n % 2], 16)
            sp.wait_ge(scr_out, NG * 32)
            for b in range(2):
                sp.wait_ge(ks_out[b], NG * 32)
                sp.wait_ge(us_out[b], NG * 32)

        @block.tensor
        def _(pe):
            pe.wait_ge(w_dve, 1)
            nc.tensor.matmul(psG[:, 0:P], wqkT4[:, 0], wqkT4[:, 1], start=True, stop=True).then_inc(w_pe, 1)
            pe.wait_ge(w_dve, 2)
            with pe.Fori(0, NG) as g:
                pe.wait_ge(xs_in, (g + 1) * 16 * G * G)
                pe.wait_ge(u_ready, g * G * NT)
                for i in range(NT):
                    if i >= 2:
                        pe.wait_ge(t2_ready, g * NT + i - 1)
                    for j in range(2):
                        for n in range(G):
                            last = nc.tensor.matmul(psA[C * n:C * n + C, i % 2, 0:TILE], lhs2[:, j, :],
                                                    xrows(XS[:, n], XTOP + TR * i, XLEFT - 1 + j),
                                                    start=(j == 0), stop=(j == 1))
                    last.then_inc(a_full, 1)

                def turn_stack(n):
                    for k in range(NT):
                        u = n * NT + k
                        pe.wait_ge(t_free, g * TSETS + max(u - 1, 0))
                        for q in range(G):
                            a = (XTOP + 2 * (G * k + q)) * XW
                            last = nc.tensor.transpose(psT[0:GR, u % 2, q * P:(q + 1) * P], XS[:, n, a:a + GR], ident[:])
                        last.then_inc(t_full, 1)

                def correlate(n):
                    pe.wait_ge(t_free, g * TSETS + (n + 1) * NT)
                    for i in range(NGR):
                        last = nc.tensor.matmul(psG[:, n * C:(n + 1) * C], TT[0:GR, n % 2, i, :], TT[0:GR, n % 2, i, 0:C],
                                                start=(i == 0), stop=(i == NGR - 1))
                    last.then_inc(gram_done, 1)

                for n in range(G + 1):
                    if n < G:
                        turn_stack(n)
                    if n >= 1:
                        correlate(n - 1)

                pe.wait_ge(lhs10_ready, g + 1)
                pe.wait_ge(t2s_in, (g + 1) * 16 * G * G)
                for i in range(NT):
                    if i >= 2:
                        pe.wait_ge(x1_ready, g * NT + i - 1)
                    for j in range(7):
                        for n in range(G):
                            o = psA[C * n:C * n + C, (NT + i) % 2, 0:TILE]
                            if j < 5:
                                w, v = lhs8[:, j, :], xrows(XS[:, n], TR * i + 2 * j, 2)
                            else:
                                w, v = lhs10[:, j - 5, n, :], yrows(T2S[:, n], TR * i + YTOP * (6 - j), YLEFT)
                            last = nc.tensor.matmul(o, w, v, start=(j == 0), stop=(j == 6))
                    last.then_inc(a_full, 1)

                pe.wait_ge(x1_ready, (g + 1) * NT)
                for k in range(NT):
                    u = G * NT + k
                    pe.wait_ge(t_free, g * TSETS + u - 1)
                    for q in range(min(G, NC - G * k)):
                        a = (G * k + q) * P
                        last = nc.tensor.transpose(psT[:, u % 2, q * P:(q + 1) * P], X1[:, a:a + P], ident[:])
                    last.then_inc(t_full, 1)

                def turn_keys(n):
                    for b in range(KSETS):
                        u = n * KSETS + b
                        pe.wait_ge(ks_ready, g * G * KSETS + max(u - 1, 0))
                        for q in range(min(8, NC - 8 * b)):
                            k = 8 * b + q
                            last = nc.tensor.transpose(psK[:, u % 2, q * P:(q + 1) * P],
                                                       Y16[:, n, k].rearrange("p s c -> p (s c)"), ident16[:])
                        last.then_inc(k_full, 1)

                def queries(n):
                    pe.wait_ge(ks_ready, (g * G + n + 1) * KSETS)
                    for i in range(NT):
                        u = n * NT + i
                        if u >= 2:
                            pe.wait_ge(u_ready, g * G * NT + u - 1)
                        nc.tensor.matmul(psA[:, u % 2, 0:TILE], mstack[:], KS[:, n % 2, i * TILE:(i + 1) * TILE],
                                         start=True, stop=True).then_inc(a_full, 1)

                pe.wait_ge(y16_ready, g + 1)
                for n in range(G + 1):
                    if n < G:
                        turn_keys(n)
                    if n >= 1:
                        queries(n - 1)

        @block.scalar
        def _(act):
            AF = 2 * NT + G * NT
            with act.Fori(0, NG) as g:
                act.wait_ge(stat_var, g + 1)
                nc.scalar.activation(rs[:], var[:], ACT.Sqrt).then_inc(stat_std, 1)
                for i in range(NT):
                    act.wait_ge(a_full, g * AF + i + 1)
                    act.wait_ge(w_zero, 2)
                    act.wait_ge(t2s_in, g * 16 * G * G)
                    nc.scalar.activation(yrows(T2[:], YTOP + TR * i, YLEFT),
                                         psA[:, i % 2, 0:TILE].rearrange("p (r w) -> p r w", w=W),
                                         ACT.Copy).then_inc(t2_ready, 1)
                for n in range(G):
                    act.wait_ge(gram_done, g * G + max(n - 1, 0))
                    for k in range(NT):
                        u = n * NT + k
                        act.wait_ge(t_full, g * TSETS + u + 1)
                        nc.scalar.activation(TT[0:GR, n % 2, G * k:G * k + G, :],
                                             psT[0:GR, u % 2].rearrange("p (q s) -> p q s", q=G),
                                             ACT.Copy).then_inc(t_free, 1)
                act.wait_ge(a_full, g * AF + 2 * NT)
                tm4 = TMf.rearrange("p (n k c) -> p n k c", n=G, k=NC)
                for k in range(NT):
                    u = G * NT + k
                    q = min(G, NC - G * k)
                    act.wait_ge(t_full, g * TSETS + u + 1)
                    nc.scalar.activation(tm4[:, :, G * k:G * k + q, :],
                                         psT[:, u % 2, 0:q * P].rearrange("p (q n c) -> p n q c", n=G, c=C),
                                         ACT.Copy).then_inc(t_free, 1)
                act.wait_ge(tm_cen, g + 1)
                nc.scalar.activation(SQf, XHf, ACT.Square).then_inc(tm_sq, 1)
                act.wait_ge(tm_var, g + 1)
                nc.scalar.activation(lrs[:], lvar[:], ACT.Sqrt).then_inc(tm_std, 1)
                for n in range(G + 1):
                    if n < G:
                        if n >= 2:
                            act.wait_ge(ks_out[n % 2], (g * 2 + 1) * 16)
                            act.wait_ge(a_full, g * AF + 2 * NT + (n - 1) * NT)
                        for b in range(KSETS):
                            u = n * KSETS + b
                            a = 8 * b * P
                            w = min(8 * P, T - a)
                            act.wait_ge(k_full, g * G * KSETS + u + 1)
                            nc.scalar.activation(KS[:, n % 2, a:a + w], psK[:, u % 2, 0:w], ACT.Copy).then_inc(ks_ready, 1)
                    if n >= 1:
                        m = n - 1
                        if m >= 2:
                            act.wait_ge(us_out[m % 2], (g * 2 + 1) * 16)
                        for i in range(NT):
                            u = m * NT + i
                            act.wait_ge(a_full, g * AF + 2 * NT + u + 1)
                            nc.scalar.activation(US[:, m % 2, i * TILE:(i + 1) * TILE], psA[:, u % 2, 0:TILE],
                                                 ACT.Copy).then_inc(u_hi, 1)

        @block.gpsimd
        def _(pool):
            with pool.Fori(0, NG) as g:
                pool.wait_ge(xh_ready, g + 1)
                nc.gpsimd.tensor_tensor(TMf, TMf, XHf, ALU.add).then_inc(res_ready, 1)

        @block.vector
        def _(dve):
            done = [0]

            def link(ins, base=None):
                done[0] += 1
                ins.then_inc(order, 1)
                dve.wait_ge(order, done[0] if link.base is None else link.base + done[0])
                return ins

            link.base = None
            nc.vector.memset(lhs2[:], 0.0)
            nc.vector.memset(wqk[:], 0.0)
            nc.vector.memset(wqk0[:], 0.0).then_inc(w_zero, 1)
            nc.vector.memset(Xp[:], 0.0)
            nc.vector.memset(X1[:, T:NC * P], 0.0)
            nc.vector.memset(gB[:], 0.0)
            nc.vector.memset(T2[:], 0.0).then_inc(w_zero, 1)
            dve.wait_ge(w_zero, 2)
            dve.wait_ge(w_in, 16 * NW)
            for i in range(5):
                nc.vector.tensor_scalar(lhs8[:, i, :], eye4[:], w8s[:, i:i + 1], None, ALU.mult)
            for i in range(2):
                link(nc.vector.tensor_scalar(p69[:, i, :], p9[:, i, :], p6[:, i:i + 1],
                                             -1.0 / math.sqrt(H * W * C * 7), ALU.mult, ALU.mult))
            link(nc.vector.tensor_tensor(wqk[:], wqk[:], wqk0[:], ALU.subtract))
            for i in range(2):
                link(nc.vector.transpose(wqkT[:, i, :], wqk[:, i, :]))
            for i in range(2):
                for s in range(G):
                    last = nc.vector.tensor_copy(wqkT4[:, i, s, :], wqkT[:, i, :])
            last.then_inc(w_dve, 1)
            dve.wait_ge(w_pe, 1)
            link(nc.vector.tensor_scalar(mfull[:], psG[:, 0:P], 1.0 / math.sqrt(C), None, ALU.mult))
            link(nc.vector.tensor_copy(mstack[:], mfull[:]))
            link(nc.vector.tensor_tensor(mstack[P // 2:P], mfull[P // 2:P], mstack[P // 2:P], ALU.subtract))
            for s in (1, 3):
                link(nc.vector.memset(mstack[C * s:C * s + 1, :], 0.0))
                link(nc.vector.memset(mstack[:, C * s:C * s + 1], 0.0))
            nc.vector.memset(tmp1[:], 0.0).then_inc(w_dve, 1)
            start = done[0]

            with dve.Fori(0, NG) as g:
                done[0] = 0
                link.base = g * ORDER + start
                dve.wait_ge(x_in, (g + 1) * 16)
                for i in range(NT):
                    last = nc.vector.bn_stats(stats[:, i, :], X1[:, i * TILE:(i + 1) * TILE])
                link(last)
                nc.vector.memset(tmp1[:], 0.0)
                link(nc.vector.bn_aggr(mv[:], stats[:].rearrange("p a b -> p (a b)")))
                nc.vector.tensor_scalar(var[:], mv[:, 1:2], GN_EPS, None, ALU.add).then_inc(stat_var, 1)
                dve.wait_ge(stat_std, g + 1)
                link(nc.vector.reciprocal(rs[:], rs[:]))
                newton_rsqrt(link, nc.vector, rs[:], var[:], tmp1[:])
                dve.wait_ge(xs_in, g * 16 * G * G)
                x3 = X1[:, 0:T].rearrange("p (r w) -> p r w", w=W)
                nc.vector.tensor_scalar(xrows(Xp[:], XTOP, XLEFT, H), x3, mv[:, 0:1], rs[:],
                                        ALU.subtract, ALU.mult).then_inc(xp_ready, 1)
                dve.wait_ge(xp_ready, g + 1)
                for i in range(5):
                    link(nc.vector.scalar_tensor_tensor(out=x3, in0=xrows(Xp[:], 2 * i, 10, H), scalar=w8e[:, i:i + 1],
                                                        in1=x3, op0=ALU.mult, op1=ALU.add))
                dve.wait_ge(t2_ready, (g + 1) * NT)
                for i in range(5):
                    link(nc.vector.scalar_tensor_tensor(out=x3, in0=yrows(T2[:], YTOP, i, H), scalar=w7e[:, i:i + 1],
                                                        in1=x3, op0=ALU.mult, op1=ALU.add))
                dve.wait_ge(gram_done, (g + 1) * G)
                link(nc.vector.tensor_copy(gsb[:].rearrange("p n c -> p (n c)"), psG[:, 0:P]))
                for n in range(G):
                    nc.vector.tensor_tensor(lhs10[:, 0, n, :], gsb[:, n, :], p69[:, 0, :], ALU.mult)
                link(nc.vector.transpose(gT[:].rearrange("p n c -> p (n c)"), gsb[:].rearrange("p n c -> p (n c)")))
                for s in range(G - 1):
                    link(nc.vector.tensor_copy(gB[C * s:C * s + C], gT[C * (G - 1 - s):C * (G - s)]))
                for n in range(G):
                    last = nc.vector.tensor_tensor(lhs10[:, 1, n, :], gB[:, n, :], p69[:, 1, :], ALU.mult)
                last.then_inc(lhs10_ready, 1)
                AF = 2 * NT + G * NT
                for i in range(NT):
                    dve.wait_ge(a_full, g * AF + NT + i + 1)
                    v = X1[:, i * TILE:(i + 1) * TILE]
                    nc.vector.tensor_tensor(v, psA[:, (NT + i) % 2, 0:TILE], v, ALU.add).then_inc(x1_ready, 1)
                def per_token(a):
                    return a[:].unsqueeze(2).broadcast_to([P, M, C])
                dve.wait_ge(t_free, (g + 1) * TSETS)
                link(nc.vector.tensor_reduce(lsum[:], TM, AX.X, ALU.add))
                link(nc.vector.tensor_scalar(lsum[:], lsum[:], 1.0 / C, None, ALU.mult))
                nc.vector.tensor_tensor(XH, TM, per_token(lsum), ALU.subtract).then_inc(tm_cen, 1)
                dve.wait_ge(tm_sq, g + 1)
                link(nc.vector.tensor_reduce(lvar[:], SQ, AX.X, ALU.add))
                nc.vector.tensor_scalar(lvar[:], lvar[:], 1.0 / C, LN_EPS, ALU.mult, ALU.add).then_inc(tm_var, 1)
                dve.wait_ge(tm_std, g + 1)
                link(nc.vector.reciprocal(lrs[:], lrs[:]))
                newton_rsqrt(link, nc.vector, lrs[:], lvar[:], ltmp[:])
                nc.vector.tensor_tensor(XH, XH, per_token(lrs), ALU.mult).then_inc(xh_ready, 1)
                dve.wait_ge(xh_ready, g + 1)
                xh4 = XHf.rearrange("p (n k c) -> p n k c", n=G, k=NC)
                link(nc.vector.tensor_copy(Y16[:, :, :, 0, :], xh4))
                nc.vector.tensor_copy(Y16[:, :, :, 2, :], Y16[:, :, :, 0, :])
                link(nc.vector.tensor_tensor(Y16[:, :, :, 1, :], xh4, Y16[:, :, :, 0, :], ALU.subtract))
                link(nc.vector.tensor_copy(Y16[:, :, :, 3, :], Y16[:, :, :, 1, :]))
                nc.vector.memset(Y16[:, :, :, :, 0:1], 1.0).then_inc(y16_ready, 1)
                dve.wait_ge(res_ready, g + 1)
                nc.vector.memset(XH[:, :, 0:1], 1.0).then_inc(val_ready, 1)
                for u in range(G * NT):
                    n, i = divmod(u, NT)
                    dve.wait_ge(u_hi, g * G * NT + u + 1)
                    v = US[P // 2:P, n % 2, i * TILE:(i + 1) * TILE]
                    nc.vector.tensor_tensor(v, psA[P // 2:P, u % 2, 0:TILE], v, ALU.subtract).then_inc(u_ready, 1)
                assert done[0] == ORDER, done[0]
def attend(nc, scr):
    with ExitStack() as ctx:
        def sb(name, shape, dt=F32):
            return ctx.enter_context(nc.sbuf_tensor("at_" + name, shape, dt))

        def ps(name, shape, dt=F32):
            return ctx.enter_context(nc.psum_tensor("at_" + name, shape, dt))

        def sem(name):
            return ctx.enter_context(nc.semaphore("at_" + name))

        TP = NC * P
        NU = NP + 1
        NQ = NC // G
        B = 3
        KS, US = sb("KS", [P, B, TP], F16), sb("US", [P, B, TP], F16)
        V = sb("V", [P, B, NC, C])
        O = sb("O", [P, B, T])
        PR = sb("PR", [P, 4, 2, TILE])
        PL = sb("PL", [P, TILE])
        XM = sb("XM", [P, NT, NC])
        negm = sb("negm", [P, NC])
        mrow = sb("mrow", [NC, 2, P], F16)
        ident = sb("ident", [P, P])
        psS = ps("psS", [P, 2, 2, 512])
        psX = ps("psX", [P, 3, 512])
        psV = ps("psV", [P, 512])

        k_in = [sem(f"k_in{b}") for b in range(B)]
        names = ("c_in zeroed s_full p_ready p_used v_full x_full x_done negm_ready mT_full mrow_ready m_in o_ready order")
        (c_in, zeroed, s_full, p_ready, p_used, v_full, x_full, x_done, negm_ready, mT_full, mrow_ready, m_in, o_ready,
         order) = map(sem, names.split())
        o_out = [sem(f"o_out{b}") for b in range(B)]
        block = ctx.enter_context(nc.Block())
        FREE_X = 4
        FREE = 2
        FULL = (N - 1) // B - 1

        def round_of(i, b):
            return i * B + b

        @block.sync
        def _(sp):
            def load(n, b):
                for dst, src in ((KS[:, b, 0:T], "ks"), (US[:, b, 0:T], "us"),
                                 (V[:, b].rearrange("p k c -> p (k c)"), "val")):
                    sp.dma_start(dst, scr[src][bass.ds(n, 1)].rearrange("a p t -> (a p) t")).then_inc(k_in[b], 16)

            def max_rows(n, b):
                sp.wait_ge(mrow_ready, n + 1)
                for h in range(2):
                    row = C * (2 * h + 1)
                    sp.dma_start(US[row:row + 1, b, :].rearrange("a (k c) -> a k c", k=NC),
                                 mrow[:, h, :]).then_inc(m_in, 16)

            def store(n, b):
                sp.wait_ge(o_ready, (n + 1) * NT)
                sp.dma_start(scr["sums"][bass.ds(n, 1)].rearrange("a p t -> (a p) t"), O[:, b]).then_inc(o_out[b], 16)

            sp.dma_start(ident[:], scr["ident"]).then_inc(c_in, 16)
            sp.wait_ge(zeroed, 1)
            for b in range(B):
                load(b, b)
            max_rows(0, 0)

            def step(n, b, more, last=False):
                if not last:
                    max_rows(n + 1, (b + 1) % B)
                store(n, b)
                if more:
                    sp.wait_ge(v_full, (n + 1) * NT)
                    load(n + B, b)

            with sp.Fori(0, FULL) as i:
                for b in range(B):
                    step(round_of(i, b), b, True)
            for n in range(FULL * B, N):
                step(n, n % B, n + B < N, n == N - 1)
            for b in range(B):
                sp.wait_ge(o_out[b], 16 * len(range(b, N, B)))

        @block.tensor
        def _(pe):
            def scores(n, b, t, u):
                base = (n * NT + t) * NU
                if u == 0:
                    pe.wait_ge(p_ready, base)
                elif u >= 2:
                    pe.wait_ge(p_ready, base + u - 1)
                chunks = (2 * u, 2 * u + 1) if u < NP else (2 * u,)
                for j, c in enumerate(chunks):
                    last = nc.tensor.matmul(psS[:, u % 2, j, 0:TILE], KS[:, b, c * P:(c + 1) * P],
                                            US[:, b, bass.ts(t, TILE)], start=True, stop=True)
                last.then_inc(s_full, 1)

            def maxima(n, b, t, c):
                base = (n * NT + t) * NC + FREE_X
                bank = 1 if c == NC - 1 else c % 3
                if c == NC - 1:
                    pe.wait_ge(x_done, base + c - 1)
                elif c == 1:
                    pe.wait_ge(x_done, base)
                else:
                    pe.wait_ge(x_done, base + c - 2 - (c == 0))
                nc.tensor.matmul(psX[:, bank, 0:TILE], US[:, b, c * P:(c + 1) * P], KS[:, b, bass.ts(t, TILE)],
                                 start=True, stop=True).then_inc(x_full, 1)

            def turn_max(n):
                pe.wait_ge(negm_ready, n + 1)
                nc.tensor.transpose(psX[0:NC, 1, 0:P], negm[:], ident[:]).then_inc(mT_full, 1)

            def sums(n, b, t, k):
                base = (n * NT + t) * NU
                if k == NQ - 1:
                    pe.wait_ge(p_ready, base + 2 * k + 2)
                if k == 0:
                    pe.wait_ge(o_ready, n * NT + t)
                for q in range(G):
                    last = nc.tensor.matmul(psV[C * q:C * q + C, 0:TILE], V[:, b, G * k + q, :],
                                            PR[:, (2 * k + q // 2) % 4, q % 2, :], start=(k == 0), stop=(k == NQ - 1))
                last.then_inc(p_used, 1)

            def last_sums(n, b, t):
                pe.wait_ge(p_ready, (n * NT + t + 1) * NU)
                QW = TILE // G
                for q in range(G):
                    last = nc.tensor.matmul(psV[C * q:C * q + C, q * QW:(q + 1) * QW], V[:, b, NC - 1, :],
                                            PL[:, q * QW:(q + 1) * QW], start=False, stop=True, skip_group_check=True)
                last.then_inc(v_full, 1)

            def tile_body(n, b, t, nxt, mx, turn=False):
                for k in range(NQ):
                    for i in range(G):
                        if i == 1 or (i == 2 and 2 * k + 3 < NU):
                            scores(n, b, t, 2 * k + i + 1)
                        if i == 3:
                            sums(n, b, t, k)
                        if mx:
                            maxima(*mx, G * k + i)
                        if turn and k == 0 and i == 0:
                            turn_max(n + 1)
                            pe.wait_ge(mrow_ready, n + 2)
                if nxt:
                    if turn:
                        pe.wait_ge(m_in, 32 * (n + 2))
                    scores(*nxt, 0)
                    scores(*nxt, 1)
                if mx:
                    maxima(*mx, NC - 1)
                last_sums(n, b, t)

            def step(n, b, ahead):
                b1, b2 = (b + 1) % B, (b + 2) % B
                with pe.Fori(0, NT - 1) as t:
                    tile_body(n, b, t, (n, b, t + 1), (n + 1, b1, t + 1) if ahead >= 1 else None)
                if ahead >= 2:
                    for s in [k_in[b2]]:
                        pe.wait_ge(s, 48 * loads(n, 2))
                tile_body(n, b, NT - 1, (n + 1, b1, 0) if ahead >= 1 else None,
                          (n + 2, b2, 0) if ahead >= 2 else None, turn=ahead >= 1)

            def loads(n, d):
                if isinstance(n, int):
                    return (n + d) // B + 1
                i, b = now
                return i + (b + d) // B + 1

            pe.wait_ge(c_in, 16)
            pe.wait_ge(zeroed, 1)
            pe.wait_ge(k_in[0], 48)
            with pe.Fori(0, NT) as t:
                for c in range(NC):
                    maxima(0, 0, t, c)
            turn_max(0)
            pe.wait_ge(k_in[1], 48)
            pe.wait_ge(mrow_ready, 1)
            for c in range(NC):
                maxima(1, 1, 0, c)
            pe.wait_ge(m_in, 32)
            scores(0, 0, 0, 0)
            scores(0, 0, 0, 1)
            with pe.Fori(0, FULL) as i:
                for b in range(B):
                    now = (i, b)
                    step(round_of(i, b), b, 2)
            for n in range(FULL * B, N):
                step(n, n % B, N - 1 - n)

        @block.scalar
        def _(act):
            def exponentials(base, j, u):
                act.wait_ge(s_full, base + u + 1)
                if u < NP:
                    if u % 2 == 0:
                        act.wait_ge(p_used, j * NQ + u // 2 - 1 + FREE)
                    nc.scalar.activation(PR[:, u % 4], psS[:, u % 2, :, 0:TILE], ACT.Exp).then_inc(p_ready, 1)
                else:
                    nc.scalar.activation(PL[0:LAST], psS[0:LAST, u % 2, 0, 0:TILE], ACT.Exp).then_inc(p_ready, 1)

            def tile_body(n, b, t, more=True):
                j = n * NT + t
                base = j * NU
                for u in range(1, NU):
                    exponentials(base, j, u)
                if more:
                    exponentials(base + NU, j + 1, 0)
                act.wait_ge(v_full, j + 1)
                nc.scalar.activation(O[:, b, bass.ts(t, TILE)], psV[:, 0:TILE], ACT.Copy).then_inc(o_ready, 1)

            act.wait_ge(zeroed, 1)
            exponentials(0, 0, 0)
            with act.Fori(0, FULL) as i:
                for b in range(B):
                    act.wait_ge(o_out[b], i * 16)
                    with act.Fori(0, NT) as t:
                        tile_body(round_of(i, b), b, t)
            for n in range(FULL * B, N):
                act.wait_ge(o_out[n % B], n // B * 16)
                with act.Fori(0, NT - 1) as t:
                    tile_body(n, n % B, t)
                tile_body(n, n % B, NT - 1, n < N - 1)

        @block.vector
        def _(dve):
            def maxima(n, t):
                base = (n * NT + t) * NC
                for c in range(NC):
                    bank = 1 if c == NC - 1 else c % 3
                    dve.wait_ge(x_full, base + c + 1)
                    nc.vector.tensor_reduce(XM[:, bass.ds(t, 1), c:c + 1], psX[:, bank, 0:TILE].unsqueeze(1),
                                            AX.X, ALU.max).then_inc(x_done, 1)

            def max_parts(n, after=None):
                dve.wait_ge(x_done, (n * NT + NT) * NC + FREE_X)
                nc.vector.tensor_reduce(negm[:], XM[:].rearrange("p t c -> p c t"), AX.X, ALU.max,
                                        negate=True).then_inc(negm_ready, 1)

            def max_halves(n):
                dve.wait_ge(mT_full, n + 1)
                dve.wait_ge(m_in, 32 * n)
                nc.vector.tensor_copy(mrow[:, 0, :], psX[0:NC, 1, 0:P]).then_inc(order, 1)
                dve.wait_ge(order, n + 1)
                nc.vector.tensor_tensor(mrow[:, 1, :], psX[0:NC, 1, 0:P], mrow[:, 0, :],
                                        ALU.subtract).then_inc(mrow_ready, 1)

            def first_maxima(n, ahead, turned):
                dve.wait_ge(negm_ready, n)
                for c in range(NC):
                    bank = 1 if c == NC - 1 else c % 3
                    dve.wait_ge(x_full, n * NT * NC + c + 1)
                    nc.vector.tensor_reduce(XM[:, 0:1, c:c + 1], psX[:, bank, 0:TILE].unsqueeze(1),
                                            AX.X, ALU.max).then_inc(x_done, 1)
                    if c == 0 and turned is not None:
                        max_halves(turned)

            def step(n, ahead):
                if ahead >= 1:
                    with dve.Fori(0, NT - 1) as t:
                        maxima(n + 1, t + 1)
                    max_parts(n + 1)
                if ahead >= 2:
                    first_maxima(n + 2, ahead, n + 1)
                elif ahead == 1:
                    max_halves(n + 1)

            nc.vector.memset(XM[:], 0.0).then_inc(x_done, FREE_X)
            nc.vector.memset(PL[:], 0.0).then_inc(p_used, FREE)
            nc.vector.memset(KS[:, :, T:TP], 0.0)
            nc.vector.memset(US[:, :, T:TP], 0.0).then_inc(zeroed, 1)
            with dve.Fori(0, NT) as t:
                maxima(0, t)
            max_parts(0)
            max_halves(0)
            first_maxima(1, 2, None)
            with dve.Fori(0, FULL) as i:
                for b in range(B):
                    step(round_of(i, b), 2)
            for n in range(FULL * B, N):
                step(n, N - 1 - n)
def finish(nc, wts, scr, out):
    with ExitStack() as ctx:
        def sb(name, shape, dt=F32):
            return ctx.enter_context(nc.sbuf_tensor("fi_" + name, shape, dt))

        def ps(name, shape, dt=F32):
            return ctx.enter_context(nc.psum_tensor("fi_" + name, shape, dt))

        def sem(name):
            return ctx.enter_context(nc.semaphore("fi_" + name))

        M = G * NC
        NU = NP + 1
        KSETS = 4
        EC = E * C
        WZ = EC + E
        ident, ident16 = sb("ident", [P, P]), sb("ident16", [P, P], F16)
        wv, wv0 = sb("wv", [P, C + 1]), sb("wv0", [P, C + 1])
        wz, wz0 = sb("wz", [P, WZ]), sb("wz0", [P, WZ])
        wz16 = sb("wz16", [P, WZ], F16)
        rev = sb("rev", [P, E])
        SUMS = sb("SUMS", [P, 2, T])
        rl = sb("rl", [P, 2, NP + 1])
        T1 = sb("T1", [P, M, C])
        RES = sb("RES", [P, M, C])
        XH, SQ = sb("XH", [P, M, C]), sb("SQ", [P, M, C])
        lsum, lvar, lrs, ltmp = (sb(n, [P, M]) for n in ("lsum", "lvar", "lrs", "ltmp"))
        Z16 = sb("Z16", [P, G, NC, G, C], F16)
        ZS = sb("ZS", [P, G, T], F16)
        LG, CAND, SEL1, SEL2, WT = (sb(n, [P, M, E]) for n in ("LG", "CAND", "SEL1", "SEL2", "WT"))
        top1, top2, cmax, g1, g2 = (sb(n, [P, M]) for n in ("top1", "top2", "cmax", "g1", "g2"))
        WE = sb("WE", [P, 3, 2, E, C])
        OUT = sb("OUT", [P, T])
        psO = ps("psO", [P, 2, 512])
        psK = ps("psK", [P, 2, 1024], F16)
        psL = ps("psL", [P, 512])
        psE = ps("psE", [P, 2, 512])

        sums_in = [sem("sums_in0"), sem("sums_in1")]
        names = ("w_in w_zero w_ready res_in o_full o_done t1_cen t1_sq t1_var t1_std z16_ready k_full zs_ready l_full "
                 "lg_done gap_ready gap_exp gates_ready e_full we_ready we_used pool_order fm_ready f_full f_done "
                 "out_done order")
        (w_in, w_zero, w_ready, res_in, o_full, o_done, t1_cen, t1_sq, t1_var, t1_std, z16_ready, k_full, zs_ready,
         l_full, lg_done, gap_ready, gap_exp, gates_ready, e_full, we_ready, we_used, pool_order, fm_ready, f_full,
         f_done, out_done, order) = map(sem, names.split())
        block = ctx.enter_context(nc.Block())
        res_g = scr["res"].rearrange("(g n) p f -> g p n f", n=G)
        out_g = out.rearrange("(g n) c h w -> g (n c) (h w)", n=G)
        FSETS = -(-NC // G)
        NW = 3 + 6 * G

        @block.sync
        def _(sp):
            sp.dma_start(ident[:], wts["ident"]).then_inc(w_in, 16)
            sp.dma_start(ident16[:], wts["ident16"]).then_inc(w_in, 16)
            sp.dma_start(rev[:], wts["rev"]).then_inc(w_in, 16)
            sp.wait_ge(w_zero, 1)
            for s in range(G):
                for dst, dst0, w, b, n in ((wv, wv0, "Wv", "bv", C), (wz, wz0, "wz", "bz", WZ)):
                    sp.dma_start(dst[C * s + 1:C * s + C, 0:n], wts[w][1:C, :]).then_inc(w_in, 16)
                    sp.dma_start(dst[C * s:C * s + 1, 0:n], wts[b]).then_inc(w_in, 16)
                    sp.dma_start(dst0[C * s + 1:C * s + C, 0:n],
                                 wts[w][0:1, :].broadcast_to([C - 1, n])).then_inc(w_in, 16)
            with sp.Fori(0, NG) as g:
                for n in range(G):
                    sp.wait_ge(o_full, g * 2 * G + 2 * max(n - 1, 0))
                    sp.dma_start(SUMS[:, n % 2], scr["sums"][bass.ds(g * G + n, 1)].rearrange(
                        "a p t -> (a p) t")).then_inc(sums_in[n % 2], 16)
                    if n == 1:
                        sp.wait_ge(fm_ready, g)
                        sp.dma_start(RES[:].rearrange("p (n k) c -> p n (k c)", n=G),
                                     res_g[bass.ds(g, 1)].rearrange("a p n f -> (a p) n f")).then_inc(res_in, 16)
                sp.wait_ge(f_done, (g + 1) * FSETS)
                sp.dma_start(out_g[bass.ds(g, 1)].rearrange("a p t -> (a p) t"), OUT[:]).then_inc(out_done, 16)
            sp.wait_ge(out_done, 16 * NG)

        @block.tensor
        def _(pe):
            pe.wait_ge(w_ready, 1)
            with pe.Fori(0, NG) as g:
                pe.wait_ge(f_done, g * FSETS)
                for n in range(G):
                    pe.wait_ge(sums_in[n % 2], (g * 2 + n // 2 + 1) * 16)
                    for h in range(2):
                        u = 2 * n + h
                        if u >= 2:
                            pe.wait_ge(o_done, g * 2 * G + u - 1)
                        for q in range(NP + h):
                            a = (h * NP + q) * P
                            w = min(P, T - a)
                            last = nc.tensor.matmul(psO[0:w, h, q * (C + 1):(q + 1) * (C + 1)], SUMS[:, n % 2, a:a + w],
                                                    wv[:], start=True, stop=True)
                        last.then_inc(o_full, 1)

                def turn_tokens(n):
                    for b in range(KSETS):
                        u = n * KSETS + b
                        pe.wait_ge(zs_ready, g * G * KSETS + max(u - 1, 0))
                        for q in range(min(8, NC - 8 * b)):
                            last = nc.tensor.transpose(psK[:, u % 2, q * P:(q + 1) * P],
                                                       Z16[:, n, 8 * b + q].rearrange("p s c -> p (s c)"), ident16[:])
                        last.then_inc(k_full, 1)

                def router(n):
                    pe.wait_ge(zs_ready, (g * G + n + 1) * KSETS)
                    pe.wait_ge(lg_done, g * G + n)
                    for k in range(NC):
                        w = min(P, T - k * P)
                        last = nc.tensor.matmul(psL[0:w, k * E:(k + 1) * E], ZS[:, n, k * P:k * P + w], wz16[:, EC:WZ],
                                                start=True, stop=True)
                    last.then_inc(l_full, 1)

                pe.wait_ge(z16_ready, g + 1)
                for n in range(G + 1):
                    if n < G:
                        turn_tokens(n)
                    if n >= 1:
                        router(n - 1)
                pe.wait_ge(gates_ready, g + 1)
                for v in range(G * NU):
                    n, u = divmod(v, NU)
                    if v >= 2:
                        pe.wait_ge(we_ready, g * G * NU + v - 1)
                    for j in range(2 if u < NP else 1):
                        a = (2 * u + j) * P
                        w = min(P, T - a)
                        last = nc.tensor.matmul(psE[0:w, v % 2, j * EC:(j + 1) * EC], ZS[:, n, a:a + w], wz16[:, 0:EC],
                                                start=True, stop=True)
                    last.then_inc(e_full, 1)
                pe.wait_ge(fm_ready, g + 1)
                for k in range(FSETS):
                    if k >= 2:
                        pe.wait_ge(f_done, g * FSETS + k - 1)
                    for q in range(min(G, NC - G * k)):
                        c = G * k + q
                        last = nc.tensor.transpose(psO[:, k % 2, q * P:(q + 1) * P],
                                                   XH[:, G * c:G * c + G, :].rearrange("p n c -> p (n c)"), ident[:])
                    last.then_inc(f_full, 1)

        @block.scalar
        def _(act):
            with act.Fori(0, NG) as g:
                act.wait_ge(t1_cen, g + 1)
                nc.scalar.activation(SQ[:], XH[:], ACT.Square).then_inc(t1_sq, 1)
                act.wait_ge(t1_var, g + 1)
                nc.scalar.activation(lrs[:], lvar[:], ACT.Sqrt).then_inc(t1_std, 1)
                for n in range(G):
                    for b in range(KSETS):
                        u = n * KSETS + b
                        a = 8 * b * P
                        w = min(8 * P, T - a)
                        act.wait_ge(k_full, g * G * KSETS + u + 1)
                        nc.scalar.activation(ZS[:, n, a:a + w], psK[:, u % 2, 0:w], ACT.Copy).then_inc(zs_ready, 1)
                act.wait_ge(gap_ready, g + 1)
                nc.scalar.activation(g2[:], top2[:], ACT.Exp).then_inc(gap_exp, 1)
                act.wait_ge(out_done, g * 16)
                for k in range(FSETS):
                    a = G * k * P
                    w = min(G * P, T - a)
                    act.wait_ge(f_full, g * FSETS + k + 1)
                    nc.scalar.activation(OUT[:, a:a + w], psO[:, k % 2, 0:w], ACT.Copy).then_inc(f_done, 1)

        @block.gpsimd
        def _(pool):
            with pool.Fori(0, NG) as g:
                for v in range(G * NU):
                    n, u = divmod(v, NU)
                    j = 2 if u < NP else 1
                    w = P if u < NP else LAST
                    e = WE[0:w, v % 3, 0:j]
                    pool.wait_ge(we_ready, g * G * NU + v + 1)
                    for i, h in enumerate((4, 2)):
                        nc.gpsimd.tensor_tensor(e[:, :, 0:h, :], e[:, :, 0:h, :], e[:, :, h:2 * h, :],
                                                ALU.add).then_inc(pool_order, 1)
                        pool.wait_ge(pool_order, g * 2 * G * NU + 2 * v + i + 1)
                    k = n * NC + 2 * u
                    nc.gpsimd.tensor_tensor(SQ[0:w, k:k + j, :], e[:, :, 0, :], e[:, :, 1, :], ALU.add).then_inc(we_used, 1)

        @block.vector
        def _(dve):
            done = [0]
            base = [0]

            def link(ins):
                done[0] += 1
                ins.then_inc(order, 1)
                dve.wait_ge(order, base[0] + done[0])

            for t in (wv, wv0, wz, wz0, T1, SQ, LG):
                last = nc.vector.memset(t[:], 0.0)
            last.then_inc(w_zero, 1)
            dve.wait_ge(w_zero, 1)
            dve.wait_ge(w_in, 16 * NW)
            link(nc.vector.tensor_tensor(wv[:], wv[:], wv0[:], ALU.subtract))
            link(nc.vector.tensor_tensor(wz[:], wz[:], wz0[:], ALU.subtract))
            for s in range(G):
                nc.vector.memset(wv[C * s:C * s + 1, C:C + 1], 1.0)
            link(nc.vector.tensor_copy(wz16[:], wz[:]))
            nc.vector.tensor_tensor(wz16[P // 2:P], wz[P // 2:P], wz16[P // 2:P], ALU.subtract).then_inc(w_ready, 1)
            start = done[0]

            def per_token(a, n=C):
                return a[:].unsqueeze(2).broadcast_to([P, M, n])

            with dve.Fori(0, NG) as g:
                done[0] = 0
                base[0] = g * ORDER_F + start
                for u in range(2 * G):
                    n, h = divmod(u, 2)
                    q = NP + h
                    dve.wait_ge(o_full, g * 2 * G + u + 1)
                    o = psO[:, h, 0:q * (C + 1)].rearrange("p (k c) -> p k c", c=C + 1)
                    k = n * NC + h * NP
                    for w, a, b in ((P, 0, q - h), (LAST, q - h, q)):
                        if a < b:
                            link(nc.vector.reciprocal(rl[0:w, h, a:b], o[0:w, a:b, C]))
                            last = nc.vector.tensor_tensor(T1[0:w, k + a:k + b, :], o[0:w, a:b, 0:C],
                                                           rl[0:w, h, a:b].unsqueeze(2).broadcast_to([w, b - a, C]), ALU.mult)
                    last.then_inc(o_done, 1)
                dve.wait_ge(o_done, (g + 1) * 2 * G)
                dve.wait_ge(res_in, (g + 1) * 16)
                link(nc.vector.tensor_tensor(T1[:], T1[:], RES[:], ALU.add))
                link(nc.vector.tensor_reduce(lsum[:], T1[:], AX.X, ALU.add))
                link(nc.vector.tensor_scalar(lsum[:], lsum[:], 1.0 / C, None, ALU.mult))
                nc.vector.tensor_tensor(XH[:], T1[:], per_token(lsum), ALU.subtract).then_inc(t1_cen, 1)
                dve.wait_ge(t1_sq, g + 1)
                link(nc.vector.tensor_reduce(lvar[:], SQ[:], AX.X, ALU.add))
                nc.vector.tensor_scalar(lvar[:], lvar[:], 1.0 / C, LN_EPS, ALU.mult, ALU.add).then_inc(t1_var, 1)
                dve.wait_ge(t1_std, g + 1)
                link(nc.vector.reciprocal(lrs[:], lrs[:]))
                newton_rsqrt(link, nc.vector, lrs[:], lvar[:], ltmp[:])
                link(nc.vector.tensor_tensor(XH[:], XH[:], per_token(lrs), ALU.mult))
                link(nc.vector.memset(XH[:, :, 0:1], 1.0))
                x4 = XH[:].rearrange("p (n k) c -> p n k c", n=G)
                link(nc.vector.tensor_copy(Z16[:, :, :, 0, :], x4))
                nc.vector.tensor_copy(Z16[:, :, :, 2, :], Z16[:, :, :, 0, :])
                link(nc.vector.tensor_tensor(Z16[:, :, :, 1, :], x4, Z16[:, :, :, 0, :], ALU.subtract))
                nc.vector.tensor_copy(Z16[:, :, :, 3, :], Z16[:, :, :, 1, :]).then_inc(z16_ready, 1)
                for n in range(G):
                    dve.wait_ge(l_full, g * G + n + 1)
                    for w, a, b in ((P, 0, NC - 1), (LAST, NC - 1, NC)):
                        last = nc.vector.tensor_copy(LG[0:w, n * NC + a:n * NC + b, :],
                                                     psL[0:w, a * E:b * E].rearrange("p (k e) -> p k e", e=E))
                    last.then_inc(lg_done, 1)
                dve.wait_ge(lg_done, (g + 1) * G)
                rev3 = rev[:].unsqueeze(1).broadcast_to([P, M, E])
                for top, sel in ((top1, SEL1), (top2, SEL2)):
                    link(nc.vector.tensor_reduce(top[:], LG[:], AX.X, ALU.max))
                    link(nc.vector.tensor_tensor(CAND[:], LG[:], per_token(top, E), ALU.is_equal))
                    link(nc.vector.tensor_tensor(CAND[:], CAND[:], rev3, ALU.mult))
                    link(nc.vector.tensor_reduce(cmax[:], CAND[:], AX.X, ALU.max))
                    link(nc.vector.tensor_tensor(sel[:], CAND[:], per_token(cmax, E), ALU.is_equal))
                    if sel is SEL1:
                        link(nc.vector.scalar_tensor_tensor(out=LG[:], in0=sel[:], scalar=-3e38, in1=LG[:], op0=ALU.mult,
                                                            op1=ALU.add))
                nc.vector.tensor_tensor(top2[:], top2[:], top1[:], ALU.subtract).then_inc(gap_ready, 1)
                dve.wait_ge(gap_exp, g + 1)
                link(nc.vector.tensor_scalar(g1[:], g2[:], 1.0, None, ALU.add))
                link(nc.vector.reciprocal(g1[:], g1[:]))
                link(nc.vector.tensor_tensor(g2[:], g2[:], g1[:], ALU.mult))
                link(nc.vector.tensor_tensor(SEL1[:], SEL1[:], per_token(g1, E), ALU.mult))
                link(nc.vector.tensor_tensor(SEL2[:], SEL2[:], per_token(g2, E), ALU.mult))
                nc.vector.tensor_tensor(WT[:], SEL1[:], SEL2[:], ALU.add).then_inc(gates_ready, 1)
                dve.wait_ge(gates_ready, g + 1)
                for v in range(G * NU):
                    n, u = divmod(v, NU)
                    j = 2 if u < NP else 1
                    w = P if u < NP else LAST
                    k = n * NC + 2 * u
                    dve.wait_ge(e_full, g * G * NU + v + 1)
                    if v >= 3:
                        dve.wait_ge(we_used, g * G * NU + v - 2)
                    nc.vector.tensor_tensor(WE[0:w, v % 3, 0:j], psE[0:w, v % 2, 0:j * EC].rearrange(
                        "p (k e c) -> p k e c", k=j, e=E), WT[0:w, k:k + j, :].unsqueeze(3).broadcast_to([w, j, E, C]),
                        ALU.mult).then_inc(we_ready, 1)
                dve.wait_ge(we_used, (g + 1) * G * NU)
                nc.vector.tensor_tensor(XH[:].rearrange("p (k n) c -> p n k c", n=G), T1[:].rearrange(
                    "p (n k) c -> p n k c", n=G), SQ[:].rearrange("p (n k) c -> p n k c", n=G),
                    ALU.add).then_inc(fm_ready, 1)
                assert done[0] == ORDER_F, done[0]


def layouts(i):
    w8, w7 = i["L0_conv_w8"][:, 0], i["L0_conv_w7"][:, 0, 0]
    p6, p9 = i["L0_conv_p6w"][0, :, :, 0], i["L0_conv_p9w"][0, 0]
    right, left = slice(G - 1, 2 * G - 1), slice(0, G)
    return {
        "ident": np.eye(P, dtype=np.float32),
        "ident16": np.eye(P, dtype=np.float16),
        "eye4": np.tile(np.eye(C, dtype=np.float32), (G, 1)),
        "rev": np.tile(np.arange(E, 0, -1, dtype=np.float32), (P, 1)),
        "w8s": w8[:, :, 0:G].transpose(2, 0, 1).reshape(P, 5),
        "w8e": np.tile(w8[:, :, G], (G, 1)),
        "w7e": np.tile(w7, (G, 1)),
        "p6": np.stack([p6[:, right].T.reshape(P), p6[:, left].T.reshape(P)], 1),
        "p9": np.concatenate([np.repeat(p9[right], C, 0), np.repeat(p9[left], C, 0)], 1),
        "w2t": i["L0_conv_w2"][:, :, 0].transpose(2, 1, 0),
        "wqk": np.concatenate([i["L1_attn_Wq"], i["L1_attn_Wk"]], 1),
        "bqk": np.concatenate([i["L1_attn_bq"], i["L1_attn_bk"]])[None],
        "Wv": i["L1_attn_Wv"],
        "bv": i["L1_attn_bv"][None],
        "wz": np.concatenate([i["L1_ffn_expert_w"].transpose(1, 0, 2).reshape(C, E * C), i["L1_ffn_router_w"]], 1),
        "bz": np.concatenate([i["L1_ffn_expert_b"].reshape(E * C), i["L1_ffn_router_b"]])[None],
    }


def kernel(**inputs):
    import concourse.bacc as bacc
    from concourse.bass_utils import run_bass_kernel_spmd

    nc = bacc.Bacc("TRN2", target_bir_lowering=False, num_devices=1)
    inputs = {n: np.asarray(a) for n, a in inputs.items()}
    arrays = {"x": inputs["x"], **layouts(inputs)}
    arrays = {n: np.ascontiguousarray(a) for n, a in arrays.items()}
    aps = {n: nc.dram_tensor(n, a.shape, mybir.dt.from_np(a.dtype), kind="ExternalInput").ap()
           for n, a in arrays.items()}
    out = nc.dram_tensor("out", (N, C, H, W), F32, kind="ExternalOutput").ap()
    build_program(nc, aps.pop("x"), aps, out)
    r = run_bass_kernel_spmd(nc, [arrays], core_ids=[0])
    return r.results[0]["out"]
```

```python
import math
from contextlib import ExitStack

import numpy as np
import concourse.bass as bass
from concourse import mybir

F32 = mybir.dt.float32
F16 = mybir.dt.float16
ALU = mybir.AluOpType
ACT = mybir.ActivationFunctionType
AX = mybir.AxisListType

N, C, H, W = 16, 32, 56, 56
P = 128
G = P // C
NG = N // G
T = H * W
TILE = 448
NT = T // TILE
TR = TILE // W
NC = -(-T // P)
LAST = T - (NC - 1) * P
NP = NC // 2
E = 8
GN_EPS, LN_EPS = 1e-5, 1e-5

XW, XTOP, XLEFT = W + 6, 4, 6
XLEN = (H + 2 * XTOP) * XW + 12
XS_LEN = XLEN - 2 * (G - 1)
YW, YTOP, YLEFT = W + 4, 3, 2
YLEN = (H + 2 * YTOP) * YW + 8
YS_LEN = (H + YTOP) * YW + 4
GR = 2 * XW
NGR = H // 2
ORDER_F = 29
ORDER = 33


def newton_rsqrt(link, eng, r, v, t):
    link(eng.tensor_tensor(t, r, r, ALU.mult))
    link(eng.tensor_tensor(t, t, v, ALU.mult))
    link(eng.tensor_scalar(t, t, -0.5, 1.5, ALU.mult, ALU.add))
    return link(eng.tensor_tensor(r, r, t, ALU.mult))


def build_program(nc, x, wts, out):
    def scratch(name, shape, dt):
        return nc.dram_tensor(name, shape, dt, kind="Internal").ap()

    scr = {
        "res": scratch("residual", (N, P, NC * C), F32),
        "val": scratch("values", (N, P, NC * C), F32),
        "ks": scratch("key_stacks", (N, P, T), F16),
        "us": scratch("query_stacks", (N, P, T), F16),
        "sums": scratch("sums", (N, P, T), F32),
        "ident": wts["ident"],
    }
    prepare(nc, x, wts, scr)
    attend(nc, scr)
    finish(nc, wts, scr, out)


def prepare(nc, x, wts, scr):
    with ExitStack() as ctx:
        def sb(name, shape, dt=F32):
            return ctx.enter_context(nc.sbuf_tensor("sb_" + name, shape, dt))

        def ps(name, shape, dt=F32):
            return ctx.enter_context(nc.psum_tensor(name, shape, dt))

        def sem(name):
            return ctx.enter_context(nc.semaphore(name))

        ident = sb("ident", [P, P])
        ident16 = sb("ident16", [P, P], F16)
        eye4 = sb("eye4", [P, C])
        w8s = sb("w8s", [P, 5])
        w8e = sb("w8e", [P, 5])
        w7e = sb("w7e", [P, 5])
        p6 = sb("p6", [P, 2])
        p9 = sb("p9", [P, 2, C])
        lhs8 = sb("lhs8", [P, 5, C])
        lhs2 = sb("lhs2", [P, 2, C])
        p69 = sb("p69", [P, 2, C])
        wqk = sb("wqk", [C, 2, C])
        wqk0 = sb("wqk0", [C, 2, C])
        wqkT = sb("wqkT", [C, 2, C])
        wqkT4 = sb("wqkT4", [C, 2, G, C])
        mfull = sb("mfull", [P, P])
        mstack = sb("mstack", [P, P], F16)
        X1 = sb("X1", [P, NC * P])
        Xp = sb("Xp", [P, XLEN])
        T2 = sb("T2", [P, YLEN])
        TT = sb("TT", [P, 2, NGR, P])
        stacks = sb("stacks", [P, G * XS_LEN])
        XS = stacks[:].rearrange("p (n l) -> p n l", n=G)
        NY = G * NC * P // 2
        Y16 = stacks[:, 0:NY].bitcast(F16).rearrange("p (n k s c) -> p n k s c", n=G, k=NC, s=G)
        KS = stacks[:, NY:NY + T].bitcast(F16).rearrange("p (b t) -> p b t", b=2)
        US = stacks[:, NY + T:NY + 2 * T].bitcast(F16).rearrange("p (b t) -> p b t", b=2)
        stacks2 = sb("stacks2", [P, G * YS_LEN])
        T2S = stacks2[:].rearrange("p (n l) -> p n l", n=G)
        NTM = G * NC * C
        TMf, XHf, SQf = (stacks2[:, i * NTM:(i + 1) * NTM] for i in range(3))
        TM, XH, SQ = (v.rearrange("p (m c) -> p m c", c=C) for v in (TMf, XHf, SQf))
        stats = sb("stats", [P, NT, 6])
        mv = sb("mv", [P, 2])
        var, rs, tmp1 = sb("var", [P, 1]), sb("rs", [P, 1]), sb("tmp1", [P, 1])
        gsb, gT, gB = sb("gsb", [P, G, C]), sb("gT", [P, G, C]), sb("gB", [P, G, C])
        lhs10 = sb("lhs10", [P, 2, G, C])
        M = G * NC
        lsum, lvar, lrs, ltmp = (sb(n, [P, M]) for n in ("lsum", "lvar", "lrs", "ltmp"))

        psA = ps("psA", [P, 2, 512])
        psT = ps("psT", [P, 2, 512])
        psG = ps("psG", [P, 512])
        psK = ps("psK", [P, 2, 1024], F16)

        names = ("w_in w_zero w_dve w_pe x_in xp_ready xs_in stat_var stat_std a_full t2_ready t2s_in t_full "
                 "t_free gram_done lhs10_ready x1_ready tm_cen tm_sq tm_var tm_std xh_ready res_ready scr_out "
                 "val_ready y16_ready k_full ks_ready ks_out0 ks_out1 u_hi u_ready us_out0 us_out1 order")
        (w_in, w_zero, w_dve, w_pe, x_in, xp_ready, xs_in, stat_var, stat_std, a_full, t2_ready, t2s_in, t_full,
         t_free, gram_done, lhs10_ready, x1_ready, tm_cen, tm_sq, tm_var, tm_std, xh_ready, res_ready, scr_out,
         val_ready, y16_ready, k_full, ks_ready, ks_out0, ks_out1, u_hi, u_ready, us_out0, us_out1, order) = map(sem, names.split())
        ks_out, us_out = (ks_out0, ks_out1), (us_out0, us_out1)
        block = ctx.enter_context(nc.Block())

        x_g = x.rearrange("(g n) c h w -> g (n c) (h w)", n=G)
        res_g = scr["res"].rearrange("(g n) p f -> g p n f", n=G)
        val_g = scr["val"].rearrange("(g n) p f -> g p n f", n=G)
        ks_i = scr["ks"].rearrange("(g n) p t -> g n p t", n=G)
        us_i = scr["us"].rearrange("(g n) p t -> g n p t", n=G)
        NW = 14
        KSETS = 4
        TSETS = G * NT + NT
        STEPS = 0

        def xrows(ap, row, col, rows=TR):
            a = row * XW + col
            return ap[..., a:a + rows * XW].rearrange("p (r w) -> p r w", w=XW)[:, :, 0:W]

        def yrows(ap, row, col, rows=TR):
            a = row * YW + col
            return ap[..., a:a + rows * YW].rearrange("p (r w) -> p r w", w=YW)[:, :, 0:W]

        @block.sync
        def _(sp):
            for dst, name in ((ident, "ident"), (ident16, "ident16"), (eye4, "eye4"), (w8s, "w8s"), (w8e, "w8e"),
                              (w7e, "w7e")):
                sp.dma_start(dst[:], wts[name]).then_inc(w_in, 16)
            sp.dma_start(p6[:], wts["p6"]).then_inc(w_in, 16)
            sp.dma_start(p9[:].rearrange("p a c -> p (a c)"), wts["p9"]).then_inc(w_in, 16)
            sp.wait_ge(w_zero, 1)
            sp.dma_start(lhs2[0:C, 0, :], wts["w2t"][0]).then_inc(w_in, 16)
            sp.dma_start(lhs2[C:2 * C, 0, :], wts["w2t"][2]).then_inc(w_in, 16)
            sp.dma_start(lhs2[0:C, 1, :], wts["w2t"][1]).then_inc(w_in, 16)
            sp.dma_start(wqk[1:C, :, :], wts["wqk"][1:C, :].rearrange("p (a c) -> p a c", a=2)).then_inc(w_in, 16)
            sp.dma_start(wqk[0:1, :, :], wts["bqk"].rearrange("p (a c) -> p a c", a=2)).then_inc(w_in, 16)
            sp.dma_start(wqk0[1:C, :, :], wts["wqk"][0:1, :].broadcast_to([C - 1, 2 * C]).rearrange(
                "p (a c) -> p a c", a=2)).then_inc(w_in, 16)
            with sp.Fori(0, NG) as g:
                sp.wait_ge(scr_out, g * 32)
                for b in range(2):
                    sp.wait_ge(ks_out[b], g * 32)
                    sp.wait_ge(us_out[b], g * 32)
                sp.dma_start(X1[:, 0:T], x_g[bass.ds(g, 1)].rearrange("a p t -> (a p) t")).then_inc(x_in, 16)
                sp.wait_ge(xp_ready, g + 1)
                for n in range(G):
                    for s in range(G):
                        sp.dma_start(XS[C * s:C * s + C, n, :],
                                     Xp[C * n:C * n + C, 2 * s:2 * s + XS_LEN]).then_inc(xs_in, 16)
                sp.wait_ge(t2_ready, NT * (g + 1))
                for n in range(G):
                    for s in range(G):
                        sp.dma_start(T2S[C * s:C * s + C, n, :],
                                     T2[C * n:C * n + C, YW * s:YW * s + YS_LEN]).then_inc(t2s_in, 16)
                sp.wait_ge(res_ready, g + 1)
                sp.dma_start(res_g[bass.ds(g, 1)].rearrange("a p n f -> (a p) n f"),
                             TMf.rearrange("p (n f) -> p n f", n=G)).then_inc(scr_out, 16)
                sp.wait_ge(val_ready, g + 1)
                sp.dma_start(val_g[bass.ds(g, 1)].rearrange("a p n f -> (a p) n f"),
                             XHf.rearrange("p (n f) -> p n f", n=G)).then_inc(scr_out, 16)
                for n in range(G):
                    sp.wait_ge(ks_ready, (g * G + n + 1) * KSETS)
                    sp.dma_start(ks_i[bass.ds(g, 1), n].rearrange("a p t -> (a p) t"), KS[:, n % 2]).then_inc(ks_out[n % 2], 16)
                    sp.wait_ge(u_ready, (g * G + n + 1) * NT)
                    sp.dma_start(us_i[bass.ds(g, 1), n].rearrange("a p t -> (a p) t"), US[:, n % 2]).then_inc(us_out[n % 2], 16)
            sp.wait_ge(scr_out, NG * 32)
            for b in range(2):
                sp.wait_ge(ks_out[b], NG * 32)
                sp.wait_ge(us_out[b], NG * 32)

        @block.tensor
        def _(pe):
            pe.wait_ge(w_dve, 1)
            nc.tensor.matmul(psG[:, 0:P], wqkT4[:, 0], wqkT4[:, 1], start=True, stop=True).then_inc(w_pe, 1)
            pe.wait_ge(w_dve, 2)
            with pe.Fori(0, NG) as g:
                pe.wait_ge(xs_in, (g + 1) * 16 * G * G)
                pe.wait_ge(u_ready, g * G * NT)
                for i in range(NT):
                    if i >= 2:
                        pe.wait_ge(t2_ready, g * NT + i - 1)
                    for j in range(2):
                        for n in range(G):
                            last = nc.tensor.matmul(psA[C * n:C * n + C, i % 2, 0:TILE], lhs2[:, j, :],
                                                    xrows(XS[:, n], XTOP + TR * i, XLEFT - 1 + j),
                                                    start=(j == 0), stop=(j == 1))
                    last.then_inc(a_full, 1)

                def turn_stack(n):
                    for k in range(NT):
                        u = n * NT + k
                        pe.wait_ge(t_free, g * TSETS + max(u - 1, 0))
                        for q in range(G):
                            a = (XTOP + 2 * (G * k + q)) * XW
                            last = nc.tensor.transpose(psT[0:GR, u % 2, q * P:(q + 1) * P], XS[:, n, a:a + GR], ident[:])
                        last.then_inc(t_full, 1)

                def correlate(n):
                    pe.wait_ge(t_free, g * TSETS + (n + 1) * NT)
                    for i in range(NGR):
                        last = nc.tensor.matmul(psG[:, n * C:(n + 1) * C], TT[0:GR, n % 2, i, :], TT[0:GR, n % 2, i, 0:C],
                                                start=(i == 0), stop=(i == NGR - 1))
                    last.then_inc(gram_done, 1)

                for n in range(G + 1):
                    if n < G:
                        turn_stack(n)
                    if n >= 1:
                        correlate(n - 1)

                pe.wait_ge(lhs10_ready, g + 1)
                pe.wait_ge(t2s_in, (g + 1) * 16 * G * G)
                for i in range(NT):
                    if i >= 2:
                        pe.wait_ge(x1_ready, g * NT + i - 1)
                    for j in range(7):
                        for n in range(G):
                            o = psA[C * n:C * n + C, (NT + i) % 2, 0:TILE]
                            if j < 5:
                                w, v = lhs8[:, j, :], xrows(XS[:, n], TR * i + 2 * j, 2)
                            else:
                                w, v = lhs10[:, j - 5, n, :], yrows(T2S[:, n], TR * i + YTOP * (6 - j), YLEFT)
                            last = nc.tensor.matmul(o, w, v, start=(j == 0), stop=(j == 6))
                    last.then_inc(a_full, 1)

                pe.wait_ge(x1_ready, (g + 1) * NT)
                for k in range(NT):
                    u = G * NT + k
                    pe.wait_ge(t_free, g * TSETS + u - 1)
                    for q in range(min(G, NC - G * k)):
                        a = (G * k + q) * P
                        last = nc.tensor.transpose(psT[:, u % 2, q * P:(q + 1) * P], X1[:, a:a + P], ident[:])
                    last.then_inc(t_full, 1)

                def turn_keys(n):
                    for b in range(KSETS):
                        u = n * KSETS + b
                        pe.wait_ge(ks_ready, g * G * KSETS + max(u - 1, 0))
                        for q in range(min(8, NC - 8 * b)):
                            k = 8 * b + q
                            last = nc.tensor.transpose(psK[:, u % 2, q * P:(q + 1) * P],
                                                       Y16[:, n, k].rearrange("p s c -> p (s c)"), ident16[:])
                        last.then_inc(k_full, 1)

                def queries(n):
                    pe.wait_ge(ks_ready, (g * G + n + 1) * KSETS)
                    for i in range(NT):
                        u = n * NT + i
                        if u >= 2:
                            pe.wait_ge(u_ready, g * G * NT + u - 1)
                        nc.tensor.matmul(psA[:, u % 2, 0:TILE], mstack[:], KS[:, n % 2, i * TILE:(i + 1) * TILE],
                                         start=True, stop=True).then_inc(a_full, 1)

                pe.wait_ge(y16_ready, g + 1)
                for n in range(G + 1):
                    if n < G:
                        turn_keys(n)
                    if n >= 1:
                        queries(n - 1)

        @block.scalar
        def _(act):
            AF = 2 * NT + G * NT
            with act.Fori(0, NG) as g:
                act.wait_ge(stat_var, g + 1)
                nc.scalar.activation(rs[:], var[:], ACT.Sqrt).then_inc(stat_std, 1)
                for i in range(NT):
                    act.wait_ge(a_full, g * AF + i + 1)
                    act.wait_ge(w_zero, 2)
                    act.wait_ge(t2s_in, g * 16 * G * G)
                    nc.scalar.activation(yrows(T2[:], YTOP + TR * i, YLEFT),
                                         psA[:, i % 2, 0:TILE].rearrange("p (r w) -> p r w", w=W),
                                         ACT.Copy).then_inc(t2_ready, 1)
                for n in range(G):
                    act.wait_ge(gram_done, g * G + max(n - 1, 0))
                    for k in range(NT):
                        u = n * NT + k
                        act.wait_ge(t_full, g * TSETS + u + 1)
                        nc.scalar.activation(TT[0:GR, n % 2, G * k:G * k + G, :],
                                             psT[0:GR, u % 2].rearrange("p (q s) -> p q s", q=G),
                                             ACT.Copy).then_inc(t_free, 1)
                act.wait_ge(a_full, g * AF + 2 * NT)
                tm4 = TMf.rearrange("p (n k c) -> p n k c", n=G, k=NC)
                for k in range(NT):
                    u = G * NT + k
                    q = min(G, NC - G * k)
                    act.wait_ge(t_full, g * TSETS + u + 1)
                    nc.scalar.activation(tm4[:, :, G * k:G * k + q, :],
                                         psT[:, u % 2, 0:q * P].rearrange("p (q n c) -> p n q c", n=G, c=C),
                                         ACT.Copy).then_inc(t_free, 1)
                act.wait_ge(tm_cen, g + 1)
                nc.scalar.activation(SQf, XHf, ACT.Square).then_inc(tm_sq, 1)
                act.wait_ge(tm_var, g + 1)
                nc.scalar.activation(lrs[:], lvar[:], ACT.Sqrt).then_inc(tm_std, 1)
                for n in range(G + 1):
                    if n < G:
                        if n >= 2:
                            act.wait_ge(ks_out[n % 2], (g * 2 + 1) * 16)
                            act.wait_ge(a_full, g * AF + 2 * NT + (n - 1) * NT)
                        for b in range(KSETS):
                            u = n * KSETS + b
                            a = 8 * b * P
                            w = min(8 * P, T - a)
                            act.wait_ge(k_full, g * G * KSETS + u + 1)
                            nc.scalar.activation(KS[:, n % 2, a:a + w], psK[:, u % 2, 0:w], ACT.Copy).then_inc(ks_ready, 1)
                    if n >= 1:
                        m = n - 1
                        if m >= 2:
                            act.wait_ge(us_out[m % 2], (g * 2 + 1) * 16)
                        for i in range(NT):
                            u = m * NT + i
                            act.wait_ge(a_full, g * AF + 2 * NT + u + 1)
                            nc.scalar.activation(US[:, m % 2, i * TILE:(i + 1) * TILE], psA[:, u % 2, 0:TILE],
                                                 ACT.Copy).then_inc(u_hi, 1)

        @block.gpsimd
        def _(pool):
            with pool.Fori(0, NG) as g:
                pool.wait_ge(xh_ready, g + 1)
                nc.gpsimd.tensor_tensor(TMf, TMf, XHf, ALU.add).then_inc(res_ready, 1)

        @block.vector
        def _(dve):
            done = [0]

            def link(ins, base=None):
                done[0] += 1
                ins.then_inc(order, 1)
                dve.wait_ge(order, done[0] if link.base is None else link.base + done[0])
                return ins

            link.base = None
            nc.vector.memset(lhs2[:], 0.0)
            nc.vector.memset(wqk[:], 0.0)
            nc.vector.memset(wqk0[:], 0.0).then_inc(w_zero, 1)
            nc.vector.memset(Xp[:], 0.0)
            nc.vector.memset(X1[:, T:NC * P], 0.0)
            nc.vector.memset(gB[:], 0.0)
            nc.vector.memset(T2[:], 0.0).then_inc(w_zero, 1)
            dve.wait_ge(w_zero, 2)
            dve.wait_ge(w_in, 16 * NW)
            for i in range(5):
                nc.vector.tensor_scalar(lhs8[:, i, :], eye4[:], w8s[:, i:i + 1], None, ALU.mult)
            for i in range(2):
                link(nc.vector.tensor_scalar(p69[:, i, :], p9[:, i, :], p6[:, i:i + 1],
                                             -1.0 / math.sqrt(H * W * C * 7), ALU.mult, ALU.mult))
            link(nc.vector.tensor_tensor(wqk[:], wqk[:], wqk0[:], ALU.subtract))
            for i in range(2):
                link(nc.vector.transpose(wqkT[:, i, :], wqk[:, i, :]))
            for i in range(2):
                for s in range(G):
                    last = nc.vector.tensor_copy(wqkT4[:, i, s, :], wqkT[:, i, :])
            last.then_inc(w_dve, 1)
            dve.wait_ge(w_pe, 1)
            link(nc.vector.tensor_scalar(mfull[:], psG[:, 0:P], 1.0 / math.sqrt(C), None, ALU.mult))
            link(nc.vector.tensor_copy(mstack[:], mfull[:]))
            link(nc.vector.tensor_tensor(mstack[P // 2:P], mfull[P // 2:P], mstack[P // 2:P], ALU.subtract))
            for s in (1, 3):
                link(nc.vector.memset(mstack[C * s:C * s + 1, :], 0.0))
                link(nc.vector.memset(mstack[:, C * s:C * s + 1], 0.0))
            nc.vector.memset(tmp1[:], 0.0).then_inc(w_dve, 1)
            start = done[0]

            with dve.Fori(0, NG) as g:
                done[0] = 0
                link.base = g * ORDER + start
                dve.wait_ge(x_in, (g + 1) * 16)
                for i in range(NT):
                    last = nc.vector.bn_stats(stats[:, i, :], X1[:, i * TILE:(i + 1) * TILE])
                link(last)
                nc.vector.memset(tmp1[:], 0.0)
                link(nc.vector.bn_aggr(mv[:], stats[:].rearrange("p a b -> p (a b)")))
                nc.vector.tensor_scalar(var[:], mv[:, 1:2], GN_EPS, None, ALU.add).then_inc(stat_var, 1)
                dve.wait_ge(stat_std, g + 1)
                link(nc.vector.reciprocal(rs[:], rs[:]))
                newton_rsqrt(link, nc.vector, rs[:], var[:], tmp1[:])
                dve.wait_ge(xs_in, g * 16 * G * G)
                x3 = X1[:, 0:T].rearrange("p (r w) -> p r w", w=W)
                nc.vector.tensor_scalar(xrows(Xp[:], XTOP, XLEFT, H), x3, mv[:, 0:1], rs[:],
                                        ALU.subtract, ALU.mult).then_inc(xp_ready, 1)
                dve.wait_ge(xp_ready, g + 1)
                for i in range(5):
                    link(nc.vector.scalar_tensor_tensor(out=x3, in0=xrows(Xp[:], 2 * i, 10, H), scalar=w8e[:, i:i + 1],
                                                        in1=x3, op0=ALU.mult, op1=ALU.add))
                dve.wait_ge(t2_ready, (g + 1) * NT)
                for i in range(5):
                    link(nc.vector.scalar_tensor_tensor(out=x3, in0=yrows(T2[:], YTOP, i, H), scalar=w7e[:, i:i + 1],
                                                        in1=x3, op0=ALU.mult, op1=ALU.add))
                dve.wait_ge(gram_done, (g + 1) * G)
                link(nc.vector.tensor_copy(gsb[:].rearrange("p n c -> p (n c)"), psG[:, 0:P]))
                for n in range(G):
                    nc.vector.tensor_tensor(lhs10[:, 0, n, :], gsb[:, n, :], p69[:, 0, :], ALU.mult)
                link(nc.vector.transpose(gT[:].rearrange("p n c -> p (n c)"), gsb[:].rearrange("p n c -> p (n c)")))
                for s in range(G - 1):
                    link(nc.vector.tensor_copy(gB[C * s:C * s + C], gT[C * (G - 1 - s):C * (G - s)]))
                for n in range(G):
                    last = nc.vector.tensor_tensor(lhs10[:, 1, n, :], gB[:, n, :], p69[:, 1, :], ALU.mult)
                last.then_inc(lhs10_ready, 1)
                AF = 2 * NT + G * NT
                for i in range(NT):
                    dve.wait_ge(a_full, g * AF + NT + i + 1)
                    v = X1[:, i * TILE:(i + 1) * TILE]
                    nc.vector.tensor_tensor(v, psA[:, (NT + i) % 2, 0:TILE], v, ALU.add).then_inc(x1_ready, 1)
                def per_token(a):
                    return a[:].unsqueeze(2).broadcast_to([P, M, C])
                dve.wait_ge(t_free, (g + 1) * TSETS)
                link(nc.vector.tensor_reduce(lsum[:], TM, AX.X, ALU.add))
                link(nc.vector.tensor_scalar(lsum[:], lsum[:], 1.0 / C, None, ALU.mult))
                nc.vector.tensor_tensor(XH, TM, per_token(lsum), ALU.subtract).then_inc(tm_cen, 1)
                dve.wait_ge(tm_sq, g + 1)
                link(nc.vector.tensor_reduce(lvar[:], SQ, AX.X, ALU.add))
                nc.vector.tensor_scalar(lvar[:], lvar[:], 1.0 / C, LN_EPS, ALU.mult, ALU.add).then_inc(tm_var, 1)
                dve.wait_ge(tm_std, g + 1)
                link(nc.vector.reciprocal(lrs[:], lrs[:]))
                newton_rsqrt(link, nc.vector, lrs[:], lvar[:], ltmp[:])
                nc.vector.tensor_tensor(XH, XH, per_token(lrs), ALU.mult).then_inc(xh_ready, 1)
                dve.wait_ge(xh_ready, g + 1)
                xh4 = XHf.rearrange("p (n k c) -> p n k c", n=G, k=NC)
                link(nc.vector.tensor_copy(Y16[:, :, :, 0, :], xh4))
                nc.vector.tensor_copy(Y16[:, :, :, 2, :], Y16[:, :, :, 0, :])
                link(nc.vector.tensor_tensor(Y16[:, :, :, 1, :], xh4, Y16[:, :, :, 0, :], ALU.subtract))
                link(nc.vector.tensor_copy(Y16[:, :, :, 3, :], Y16[:, :, :, 1, :]))
                nc.vector.memset(Y16[:, :, :, :, 0:1], 1.0).then_inc(y16_ready, 1)
                dve.wait_ge(res_ready, g + 1)
                nc.vector.memset(XH[:, :, 0:1], 1.0).then_inc(val_ready, 1)
                for u in range(G * NT):
                    n, i = divmod(u, NT)
                    dve.wait_ge(u_hi, g * G * NT + u + 1)
                    v = US[P // 2:P, n % 2, i * TILE:(i + 1) * TILE]
                    nc.vector.tensor_tensor(v, psA[P // 2:P, u % 2, 0:TILE], v, ALU.subtract).then_inc(u_ready, 1)
                assert done[0] == ORDER, done[0]
def attend(nc, scr):
    with ExitStack() as ctx:
        def sb(name, shape, dt=F32):
            return ctx.enter_context(nc.sbuf_tensor("at_" + name, shape, dt))

        def ps(name, shape, dt=F32):
            return ctx.enter_context(nc.psum_tensor("at_" + name, shape, dt))

        def sem(name):
            return ctx.enter_context(nc.semaphore("at_" + name))

        TP = NC * P
        NU = NP + 1
        NQ = NC // G
        B = 3
        KS, US = sb("KS", [P, B, TP], F16), sb("US", [P, B, TP], F16)
        V = sb("V", [P, B, NC, C])
        O = sb("O", [P, B, T])
        PR = sb("PR", [P, 4, 2, TILE])
        PL = sb("PL", [P, TILE])
        XM = sb("XM", [P, NT, NC])
        negm = sb("negm", [P, NC])
        mrow = sb("mrow", [NC, 2, P], F16)
        ident = sb("ident", [P, P])
        psS = ps("psS", [P, 2, 2, 512])
        psX = ps("psX", [P, 3, 512])
        psV = ps("psV", [P, 512])

        k_in = [sem(f"k_in{b}") for b in range(B)]
        names = ("c_in zeroed s_full p_ready p_used v_full x_full x_done negm_ready mT_full mrow_ready m_in o_ready order")
        (c_in, zeroed, s_full, p_ready, p_used, v_full, x_full, x_done, negm_ready, mT_full, mrow_ready, m_in, o_ready,
         order) = map(sem, names.split())
        o_out = [sem(f"o_out{b}") for b in range(B)]
        block = ctx.enter_context(nc.Block())
        FREE_X = 4
        FREE = 2
        FULL = (N - 1) // B - 1

        def round_of(i, b):
            return i * B + b

        @block.sync
        def _(sp):
            def load(n, b):
                for dst, src in ((KS[:, b, 0:T], "ks"), (US[:, b, 0:T], "us"),
                                 (V[:, b].rearrange("p k c -> p (k c)"), "val")):
                    sp.dma_start(dst, scr[src][bass.ds(n, 1)].rearrange("a p t -> (a p) t")).then_inc(k_in[b], 16)

            def max_rows(n, b):
                sp.wait_ge(mrow_ready, n + 1)
                for h in range(2):
                    row = C * (2 * h + 1)
                    sp.dma_start(US[row:row + 1, b, :].rearrange("a (k c) -> a k c", k=NC),
                                 mrow[:, h, :]).then_inc(m_in, 16)

            def store(n, b):
                sp.wait_ge(o_ready, (n + 1) * NT)
                sp.dma_start(scr["sums"][bass.ds(n, 1)].rearrange("a p t -> (a p) t"), O[:, b]).then_inc(o_out[b], 16)

            sp.dma_start(ident[:], scr["ident"]).then_inc(c_in, 16)
            sp.wait_ge(zeroed, 1)
            for b in range(B):
                load(b, b)
            max_rows(0, 0)

            def step(n, b, more, last=False):
                if not last:
                    max_rows(n + 1, (b + 1) % B)
                store(n, b)
                if more:
                    sp.wait_ge(v_full, (n + 1) * NT)
                    load(n + B, b)

            with sp.Fori(0, FULL) as i:
                for b in range(B):
                    step(round_of(i, b), b, True)
            for n in range(FULL * B, N):
                step(n, n % B, n + B < N, n == N - 1)
            for b in range(B):
                sp.wait_ge(o_out[b], 16 * len(range(b, N, B)))

        @block.tensor
        def _(pe):
            def scores(n, b, t, u):
                base = (n * NT + t) * NU
                if u == 0:
                    pe.wait_ge(p_ready, base)
                elif u >= 2:
                    pe.wait_ge(p_ready, base + u - 1)
                chunks = (2 * u, 2 * u + 1) if u < NP else (2 * u,)
                for j, c in enumerate(chunks):
                    last = nc.tensor.matmul(psS[:, u % 2, j, 0:TILE], KS[:, b, c * P:(c + 1) * P],
                                            US[:, b, bass.ts(t, TILE)], start=True, stop=True)
                last.then_inc(s_full, 1)

            def maxima(n, b, t, c):
                base = (n * NT + t) * NC + FREE_X
                bank = 1 if c == NC - 1 else c % 3
                if c == NC - 1:
                    pe.wait_ge(x_done, base + c - 1)
                elif c == 1:
                    pe.wait_ge(x_done, base)
                else:
                    pe.wait_ge(x_done, base + c - 2 - (c == 0))
                nc.tensor.matmul(psX[:, bank, 0:TILE], US[:, b, c * P:(c + 1) * P], KS[:, b, bass.ts(t, TILE)],
                                 start=True, stop=True).then_inc(x_full, 1)

            def turn_max(n):
                pe.wait_ge(negm_ready, n + 1)
                nc.tensor.transpose(psX[0:NC, 1, 0:P], negm[:], ident[:]).then_inc(mT_full, 1)

            def sums(n, b, t, k):
                base = (n * NT + t) * NU
                if k == NQ - 1:
                    pe.wait_ge(p_ready, base + 2 * k + 2)
                if k == 0:
                    pe.wait_ge(o_ready, n * NT + t)
                for q in range(G):
                    last = nc.tensor.matmul(psV[C * q:C * q + C, 0:TILE], V[:, b, G * k + q, :],
                                            PR[:, (2 * k + q // 2) % 4, q % 2, :], start=(k == 0), stop=(k == NQ - 1))
                last.then_inc(p_used, 1)

            def last_sums(n, b, t):
                pe.wait_ge(p_ready, (n * NT + t + 1) * NU)
                QW = TILE // G
                for q in range(G):
                    last = nc.tensor.matmul(psV[C * q:C * q + C, q * QW:(q + 1) * QW], V[:, b, NC - 1, :],
                                            PL[:, q * QW:(q + 1) * QW], start=False, stop=True, skip_group_check=True)
                last.then_inc(v_full, 1)

            def tile_body(n, b, t, nxt, mx, turn=False):
                for k in range(NQ):
                    for i in range(G):
                        if i == 1 or (i == 2 and 2 * k + 3 < NU):
                            scores(n, b, t, 2 * k + i + 1)
                        if i == 3:
                            sums(n, b, t, k)
                        if mx:
                            maxima(*mx, G * k + i)
                        if turn and k == 0 and i == 0:
                            turn_max(n + 1)
                            pe.wait_ge(mrow_ready, n + 2)
                if nxt:
                    if turn:
                        pe.wait_ge(m_in, 32 * (n + 2))
                    scores(*nxt, 0)
                    scores(*nxt, 1)
                if mx:
                    maxima(*mx, NC - 1)
                last_sums(n, b, t)

            def step(n, b, ahead):
                b1, b2 = (b + 1) % B, (b + 2) % B
                with pe.Fori(0, NT - 1) as t:
                    tile_body(n, b, t, (n, b, t + 1), (n + 1, b1, t + 1) if ahead >= 1 else None)
                if ahead >= 2:
                    for s in [k_in[b2]]:
                        pe.wait_ge(s, 48 * loads(n, 2))
                tile_body(n, b, NT - 1, (n + 1, b1, 0) if ahead >= 1 else None,
                          (n + 2, b2, 0) if ahead >= 2 else None, turn=ahead >= 1)

            def loads(n, d):
                if isinstance(n, int):
                    return (n + d) // B + 1
                i, b = now
                return i + (b + d) // B + 1

            pe.wait_ge(c_in, 16)
            pe.wait_ge(zeroed, 1)
            pe.wait_ge(k_in[0], 48)
            with pe.Fori(0, NT) as t:
                for c in range(NC):
                    maxima(0, 0, t, c)
            turn_max(0)
            pe.wait_ge(k_in[1], 48)
            pe.wait_ge(mrow_ready, 1)
            for c in range(NC):
                maxima(1, 1, 0, c)
            pe.wait_ge(m_in, 32)
            scores(0, 0, 0, 0)
            scores(0, 0, 0, 1)
            with pe.Fori(0, FULL) as i:
                for b in range(B):
                    now = (i, b)
                    step(round_of(i, b), b, 2)
            for n in range(FULL * B, N):
                step(n, n % B, N - 1 - n)

        @block.scalar
        def _(act):
            def exponentials(base, j, u):
                act.wait_ge(s_full, base + u + 1)
                if u < NP:
                    if u % 2 == 0:
                        act.wait_ge(p_used, j * NQ + u // 2 - 1 + FREE)
                    nc.scalar.activation(PR[:, u % 4], psS[:, u % 2, :, 0:TILE], ACT.Exp).then_inc(p_ready, 1)
                else:
                    nc.scalar.activation(PL[0:LAST], psS[0:LAST, u % 2, 0, 0:TILE], ACT.Exp).then_inc(p_ready, 1)

            def tile_body(n, b, t, more=True):
                j = n * NT + t
                base = j * NU
                for u in range(1, NU):
                    exponentials(base, j, u)
                if more:
                    exponentials(base + NU, j + 1, 0)
                act.wait_ge(v_full, j + 1)
                nc.scalar.activation(O[:, b, bass.ts(t, TILE)], psV[:, 0:TILE], ACT.Copy).then_inc(o_ready, 1)

            act.wait_ge(zeroed, 1)
            exponentials(0, 0, 0)
            with act.Fori(0, FULL) as i:
                for b in range(B):
                    act.wait_ge(o_out[b], i * 16)
                    with act.Fori(0, NT) as t:
                        tile_body(round_of(i, b), b, t)
            for n in range(FULL * B, N):
                act.wait_ge(o_out[n % B], n // B * 16)
                with act.Fori(0, NT - 1) as t:
                    tile_body(n, n % B, t)
                tile_body(n, n % B, NT - 1, n < N - 1)

        @block.vector
        def _(dve):
            def maxima(n, t):
                base = (n * NT + t) * NC
                for c in range(NC):
                    bank = 1 if c == NC - 1 else c % 3
                    dve.wait_ge(x_full, base + c + 1)
                    nc.vector.tensor_reduce(XM[:, bass.ds(t, 1), c:c + 1], psX[:, bank, 0:TILE].unsqueeze(1),
                                            AX.X, ALU.max).then_inc(x_done, 1)

            def max_parts(n, after=None):
                dve.wait_ge(x_done, (n * NT + NT) * NC + FREE_X)
                nc.vector.tensor_reduce(negm[:], XM[:].rearrange("p t c -> p c t"), AX.X, ALU.max,
                                        negate=True).then_inc(negm_ready, 1)

            def max_halves(n):
                dve.wait_ge(mT_full, n + 1)
                dve.wait_ge(m_in, 32 * n)
                nc.vector.tensor_copy(mrow[:, 0, :], psX[0:NC, 1, 0:P]).then_inc(order, 1)
                dve.wait_ge(order, n + 1)
                nc.vector.tensor_tensor(mrow[:, 1, :], psX[0:NC, 1, 0:P], mrow[:, 0, :],
                                        ALU.subtract).then_inc(mrow_ready, 1)

            def first_maxima(n, ahead, turned):
                dve.wait_ge(negm_ready, n)
                for c in range(NC):
                    bank = 1 if c == NC - 1 else c % 3
                    dve.wait_ge(x_full, n * NT * NC + c + 1)
                    nc.vector.tensor_reduce(XM[:, 0:1, c:c + 1], psX[:, bank, 0:TILE].unsqueeze(1),
                                            AX.X, ALU.max).then_inc(x_done, 1)
                    if c == 0 and turned is not None:
                        max_halves(turned)

            def step(n, ahead):
                if ahead >= 1:
                    with dve.Fori(0, NT - 1) as t:
                        maxima(n + 1, t + 1)
                    max_parts(n + 1)
                if ahead >= 2:
                    first_maxima(n + 2, ahead, n + 1)
                elif ahead == 1:
                    max_halves(n + 1)

            nc.vector.memset(XM[:], 0.0).then_inc(x_done, FREE_X)
            nc.vector.memset(PL[:], 0.0).then_inc(p_used, FREE)
            nc.vector.memset(KS[:, :, T:TP], 0.0)
            nc.vector.memset(US[:, :, T:TP], 0.0).then_inc(zeroed, 1)
            with dve.Fori(0, NT) as t:
                maxima(0, t)
            max_parts(0)
            max_halves(0)
            first_maxima(1, 2, None)
            with dve.Fori(0, FULL) as i:
                for b in range(B):
                    step(round_of(i, b), 2)
            for n in range(FULL * B, N):
                step(n, N - 1 - n)
def finish(nc, wts, scr, out):
    with ExitStack() as ctx:
        def sb(name, shape, dt=F32):
            return ctx.enter_context(nc.sbuf_tensor("fi_" + name, shape, dt))

        def ps(name, shape, dt=F32):
            return ctx.enter_context(nc.psum_tensor("fi_" + name, shape, dt))

        def sem(name):
            return ctx.enter_context(nc.semaphore("fi_" + name))

        TP = NC * P
        NU = NP + 1
        KSETS = 4
        QSETS = -(-NC // G)
        EC = E * C
        WZ = EC + E
        ident, ident16 = sb("ident", [P, P]), sb("ident16", [P, P], F16)
        wv, wv0 = sb("wv", [P, C + 1]), sb("wv0", [P, C + 1])
        wz, wz0 = sb("wz", [P, WZ]), sb("wz0", [P, WZ])
        wz16 = sb("wz16", [P, WZ], F16)
        rev = sb("rev", [P, E])
        SUMS = sb("SUMS", [P, 2, TP])
        RES = sb("RES", [P, 2, NC, C])
        ZS = sb("ZS", [P, 2, TP], F16)
        WT = sb("WT", [P, 2, NC, E])
        OUT = sb("OUT", [P, 2, QSETS * P])
        T1 = sb("T1", [P, 4, NC, C])
        rl = sb("rl", [P, 2, NP + 1])
        XH, SQ = sb("XH", [P, NC, C]), sb("SQ", [P, NC, C])
        lsum, lvar, lrs, ltmp = (sb(n, [P, NC]) for n in ("lsum", "lvar", "lrs", "ltmp"))
        Z16 = sb("Z16", [P, NC, G, C], F16)
        LG, CAND, SEL1, SEL2 = (sb(n, [P, NC, E]) for n in ("LG", "CAND", "SEL1", "SEL2"))
        top1, top2, cmax, gap, g1, g2 = (sb(n, [P, NC]) for n in ("top1", "top2", "cmax", "gap", "g1", "g2"))
        WE = sb("WE", [P, QSETS, E, G, C])
        psO = ps("psO", [P, 2, 512])
        psK = ps("psK", [P, 2, 1024], F16)
        psE = ps("psE", [P, 2, 512])
        psB = ps("psB", [P, 2, 512])
        psL = psB[:, 1, 0:NC * E]

        names = ("w_in w_zero w_ready o_full o_done t1_ready t1_cen t1_sq t1_var t1_std xh_ready z_high z16_ready k_full zs_ready "
                 "l_full lg_ready gap_ready gap_exp gates_ready e_full we_ready half_folded folded set_done out_ready order")
        (w_in, w_zero, w_ready, o_full, o_done, t1_ready, t1_cen, t1_sq, t1_var, t1_std, xh_ready, z_high, z16_ready, k_full, zs_ready,
         l_full, lg_ready, gap_ready, gap_exp, gates_ready, e_full, we_ready, half_folded, folded, set_done, out_ready,
         order) = map(sem, names.split())
        sums_in, res_in, out_done = ([sem(f"{s}{b}") for b in range(2)] for s in ("sums_in", "res_in", "out_done"))
        block = ctx.enter_context(nc.Block())
        NW = 3 + 6 * G
        STORES = 16 * (G + 1)
        FIRST, TURN = 3, 4
        assert N % TURN == 0

        def steps(eng, step):
            for n in range(FIRST):
                step(n, n % TURN, n // 2)
            with eng.Fori(0, (N - TURN) // TURN) as i:
                for n in range(FIRST, FIRST + TURN):
                    step(i * TURN + n, n % TURN, i * 2 + n // 2)
            for n in range(N - 1, N + 1):
                step(n, n % TURN, n // 2)

        def beyond(n, k):
            return not isinstance(n, int) or n > k

        @block.sync
        def _(sp):
            def load(n, b):
                if beyond(n, 1):
                    sp.wait_ge(o_full, n * 2 - 2)
                sp.dma_start(SUMS[:, b, 0:T], scr["sums"][bass.ds(n, 1)].rearrange(
                    "a p t -> (a p) t")).then_inc(sums_in[b], 16)
                if beyond(n, 1):
                    sp.wait_ge(t1_ready, n - 1)
                sp.dma_start(RES[:, b].rearrange("p k c -> p (k c)"), scr["res"][bass.ds(n, 1)].rearrange(
                    "a p f -> (a p) f")).then_inc(res_in[b], 16)

            def store(n, b):
                o = out[bass.ds(n, 1)].rearrange("a c h w -> (a c) (h w)")
                full = QSETS - 1
                sp.wait_ge(out_ready, n + 1)
                for q in range(G):
                    sp.dma_start(o[:, 0:full * G * P].rearrange("c (k q p) -> c k q p", q=G, p=P)[:, :, q],
                                 OUT[C * q:C * q + C, b, 0:full * P].rearrange("c (k p) -> c k p", p=P)).then_inc(
                                     out_done[b], 16)
                sp.dma_start(o[:, full * G * P:T], OUT[0:C, b, full * P:full * P + LAST]).then_inc(out_done[b], 16)

            def step(n, c, r):
                b = c % 2
                if not isinstance(n, int) or n + 1 < N:
                    load(n + 1, 1 - b)
                if beyond(n, 1):
                    store(n - 2, b)

            sp.dma_start(ident[:], wts["ident"]).then_inc(w_in, 16)
            sp.dma_start(ident16[:], wts["ident16"]).then_inc(w_in, 16)
            sp.dma_start(rev[:], wts["rev"]).then_inc(w_in, 16)
            load(0, 0)
            sp.wait_ge(w_zero, 1)
            for s in range(G):
                for dst, dst0, w, b, n in ((wv, wv0, "Wv", "bv", C), (wz, wz0, "wz", "bz", WZ)):
                    sp.dma_start(dst[C * s + 1:C * s + C, 0:n], wts[w][1:C, :]).then_inc(w_in, 16)
                    sp.dma_start(dst[C * s:C * s + 1, 0:n], wts[b]).then_inc(w_in, 16)
                    sp.dma_start(dst0[C * s + 1:C * s + C, 0:n],
                                 wts[w][0:1, :].broadcast_to([C - 1, n])).then_inc(w_in, 16)
            steps(sp, step)
            store(N - 1, 1)
            for b in range(2):
                sp.wait_ge(out_done[b], STORES * (N // 2))

        @block.tensor
        def _(pe):
            def project(n, b, r, halves):
                for h in halves:
                    if h == 0:
                        pe.wait_ge(sums_in[b], (r + 1) * 16)
                    if beyond(n, 0):
                        pe.wait_ge(o_done, n * 2 + h - 1)
                    for q in range(NP + h):
                        a = (h * NP + q) * P
                        last = nc.tensor.matmul(psO[:, h, q * (C + 1):(q + 1) * (C + 1)], SUMS[:, b, a:a + P],
                                                wv[:], start=True, stop=True)
                    last.then_inc(o_full, 1)

            def turn_tokens(n, s):
                if beyond(n, 0) or s >= 2:
                    pe.wait_ge(zs_ready, n * KSETS + s - 1)
                for q in range(min(8, NC - 8 * s)):
                    last = nc.tensor.transpose(psK[:, s % 2, q * P:(q + 1) * P],
                                               Z16[:, 8 * s + q].rearrange("p s c -> p (s c)"), ident16[:])
                last.then_inc(k_full, 1)

            def router(n, b):
                pe.wait_ge(zs_ready, n * KSETS + KSETS)
                if beyond(n, 1):
                    pe.wait_ge(out_ready, n - 1)
                for k in range(NC):
                    last = nc.tensor.matmul(psL[:, k * E:(k + 1) * E], ZS[:, b, k * P:(k + 1) * P], wz16[:, EC:WZ],
                                            start=True, stop=True)
                last.then_inc(l_full, 1)

            def experts(n, b, units):
                for u in units:
                    if beyond(n, 0) or u >= 2:
                        pe.wait_ge(we_ready, n * NU + (u - 1 if u >= 2 else -u))
                    for j in range(2 if u < NP else 1):
                        a = (2 * u + j) * P
                        last = nc.tensor.matmul(psE[:, u % 2, j * EC:(j + 1) * EC], ZS[:, b, a:a + P], wz16[:, 0:EC],
                                                start=True, stop=True)
                    last.then_inc(e_full, 1)

            def sums(n, c):
                for s in range(QSETS):
                    pe.wait_ge(folded, n * QSETS + s + 1)
                    if s == 0 and beyond(n, 0):
                        pe.wait_ge(out_ready, n)
                    if s == 4 and (not isinstance(n, int) or n + 1 < N):
                        pe.wait_ge(lg_ready, n + 2)
                    w = min(G, NC - G * s) * C
                    for e in range(E // 4 + 1):
                        v = (WE[:, s, e] if e < E // 4 else T1[:, c, G * s:G * s + w // C]).rearrange("p q c -> p (q c)")
                        last = nc.tensor.matmul(psB[0:w, s // 4, s % 4 * P:(s % 4 + 1) * P], v[:, 0:w], ident[:],
                                                start=(e == 0), stop=(e == E // 4))
                    last.then_inc(set_done, 1)

            def step(n, c, r):
                b = c % 2
                m, mb, mc = n - 1, 1 - b, (c - 1) % TURN
                old = beyond(n, 0)
                new = not isinstance(n, int) or n < N
                more = not isinstance(n, int) or n + 1 < N
                if more:
                    project(n + 1, mb, r + b, (0,))
                if old:
                    experts(m, mb, (2, 3, 4))
                if more:
                    project(n + 1, mb, r + b, (1,))
                if old:
                    experts(m, mb, (5, 6))
                if new:
                    pe.wait_ge(z16_ready, n + 1)
                    pe.wait_ge(z_high, n * 2 + 2)
                for s in range(KSETS):
                    if new:
                        turn_tokens(n, s)
                    if old:
                        experts(m, mb, (s + 7,))
                if new:
                    router(n, b)
                if old:
                    experts(m, mb, (11, 12))
                if new:
                    experts(n, b, (0, 1))
                if old:
                    sums(m, mc)

            pe.wait_ge(w_ready, 1)
            project(0, 0, 0, (0, 1))
            steps(pe, step)

        @block.scalar
        def _(act):
            def to_image(n, b, r):
                act.wait_ge(set_done, n * QSETS + QSETS)
                if beyond(n, 1):
                    act.wait_ge(out_done[b], r * STORES)
                nc.scalar.activation(OUT[:, b, 0:4 * P], psB[:, 0], ACT.Copy)
                nc.scalar.activation(OUT[:, b, 4 * P:6 * P], psB[:, 1, 0:2 * P], ACT.Copy)
                nc.scalar.activation(OUT[0:C, b, 6 * P:7 * P], psB[0:C, 1, 2 * P:3 * P], ACT.Copy).then_inc(out_ready, 1)

            def step(n, c, r):
                b = c % 2
                if not isinstance(n, int) or n < N:
                    act.wait_ge(t1_cen, n + 1)
                    nc.scalar.activation(SQ[:], XH[:], ACT.Square).then_inc(t1_sq, 1)
                    act.wait_ge(t1_var, n + 1)
                    nc.scalar.activation(lrs[:], lvar[:], ACT.Sqrt).then_inc(t1_std, 1)
                if beyond(n, 1):
                    to_image(n - 2, b, r - 1)
                if not isinstance(n, int) or n < N:
                    act.wait_ge(xh_ready, n + 1)
                    if beyond(n, 0):
                        act.wait_ge(k_full, n * KSETS)
                    for s in (0, 2):
                        nc.scalar.activation(Z16[:, :, s, :], XH[:], ACT.Copy).then_inc(z_high, 1)
                    for s in range(KSETS):
                        a = 8 * s * P
                        w = min(8 * P, TP - a)
                        act.wait_ge(k_full, n * KSETS + s + 1)
                        if s == 0 and beyond(n, 1):
                            act.wait_ge(e_full, n * NU - NU)
                        nc.scalar.activation(ZS[:, b, a:a + w], psK[:, s % 2, 0:w], ACT.Copy).then_inc(zs_ready, 1)
                    act.wait_ge(l_full, n + 1)
                    nc.scalar.activation(LG[:].rearrange("p k e -> p (k e)"), psL, ACT.Copy).then_inc(lg_ready, 1)
                    act.wait_ge(gap_ready, n + 1)
                    nc.scalar.activation(g2[:], gap[:], ACT.Exp).then_inc(gap_exp, 1)
            steps(act, step)
            to_image(N - 1, 1, (N - 1) // 2)

        @block.gpsimd
        def _(pool):
            def fold(s, h):
                w = min(G, NC - G * s)
                return nc.gpsimd.tensor_tensor(WE[:, s, 0:h, 0:w], WE[:, s, 0:h, 0:w], WE[:, s, h:2 * h, 0:w], ALU.add)

            def residual(n, c, r):
                b = c % 2
                pool.wait_ge(o_done, n * 2 + 2)
                pool.wait_ge(res_in[b], (r + 1) * 16)
                nc.gpsimd.tensor_tensor(T1[:, c], T1[:, c], RES[:, b], ALU.add).then_inc(t1_ready, 1)

            def step(n, c, r):
                b = c % 2
                if beyond(n, 0):
                    for s in range(QSETS + 1):
                        if s < QSETS:
                            pool.wait_ge(we_ready, n * NU - NU + min(2 * s + 2, NU))
                            fold(s, E // 2).then_inc(half_folded, 1)
                        if s >= 1:
                            pool.wait_ge(half_folded, n * QSETS - QSETS + s)
                            fold(s - 1, E // 4).then_inc(folded, 1)
                if not isinstance(n, int) or n + 1 < N:
                    residual(n + 1, (c + 1) % TURN, r + b)

            residual(0, 0, 0)
            steps(pool, step)

        @block.vector
        def _(dve):
            done = [0]
            base = [0]

            def mark(ins):
                done[0] += 1
                return ins.then_inc(order, 1)

            def settled():
                dve.wait_ge(order, base[0] + done[0])

            def link(ins):
                mark(ins)
                settled()

            def per_token(a, n=C):
                return a.unsqueeze(2).broadcast_to([P, a.shape[1], n])

            def weigh(n, b, units):
                if n is None:
                    return
                for u in units:
                    j = 2 if u < NP else 1
                    dve.wait_ge(e_full, n * NU + u + 1)
                    if u % 2 == 0 and beyond(n, 0):
                        dve.wait_ge(set_done, n * QSETS - QSETS + u // 2 + 1)
                    q = u % 2 * 2
                    nc.vector.tensor_tensor(WE[:, u // 2, :, q:q + j].rearrange("p e k c -> p k e c"), psE[:, u % 2, 0:j * EC].rearrange(
                        "p (k e c) -> p k e c", k=j, e=E), WT[:, b, 2 * u:2 * u + j, :].unsqueeze(3).broadcast_to(
                            [P, j, E, C]), ALU.mult).then_inc(we_ready, 1)

            def o_part(h):
                q = NP + h
                return psO[:, h, 0:q * (C + 1)].rearrange("p (k c) -> p k c", c=C + 1), rl[:, h, 0:q]

            def invert(n, h):
                o, r = o_part(h)
                dve.wait_ge(o_full, n * 2 + h + 1)
                mark(nc.vector.reciprocal(r, o[:, :, C]))

            def divide(n, c, h):
                o, r = o_part(h)
                nc.vector.tensor_tensor(T1[:, c, h * NP:h * NP + NP + h, :], o[:, :, 0:C], per_token(r),
                                        ALU.mult).then_inc(o_done, 1)

            def step(n, c, r):
                b = c % 2
                new = not isinstance(n, int) or n < N
                m, mb = (n - 1, 1 - b) if beyond(n, 0) else (None, None)
                if not new:
                    weigh(m, mb, range(NU))
                    return
                done[0] = 0
                base[0] = n * ORDER_F + start
                weigh(m, mb, (0,))
                dve.wait_ge(t1_ready, n + 1)
                mark(nc.vector.tensor_reduce(lsum[:], T1[:, c], AX.X, ALU.add))
                settled()
                mark(nc.vector.tensor_scalar(lsum[:], lsum[:], 1.0 / C, None, ALU.mult))
                weigh(m, mb, (1,))
                settled()
                nc.vector.tensor_tensor(XH[:], T1[:, c], per_token(lsum[:]), ALU.subtract).then_inc(t1_cen, 1)
                weigh(m, mb, (2,))
                dve.wait_ge(t1_sq, n + 1)
                link(nc.vector.tensor_reduce(lvar[:], SQ[:], AX.X, ALU.add))
                nc.vector.tensor_scalar(lvar[:], lvar[:], 1.0 / C, LN_EPS, ALU.mult, ALU.add).then_inc(t1_var, 1)
                weigh(m, mb, (3, 4))
                dve.wait_ge(t1_std, n + 1)
                link(nc.vector.reciprocal(lrs[:], lrs[:]))
                newton_rsqrt(link, nc.vector, lrs[:], lvar[:], ltmp[:])
                link(nc.vector.tensor_tensor(XH[:], XH[:], per_token(lrs[:]), ALU.mult))
                nc.vector.memset(XH[:, :, 0:1], 1.0).then_inc(xh_ready, 1)
                dve.wait_ge(z_high, n * 2 + 1)
                mark(nc.vector.tensor_tensor(Z16[:, :, 1, :], XH[:], Z16[:, :, 0, :], ALU.subtract))
                settled()
                nc.vector.tensor_copy(Z16[:, :, 3, :], Z16[:, :, 1, :]).then_inc(z16_ready, 1)
                weigh(m, mb, range(5, NU))
                dve.wait_ge(lg_ready, n + 1)
                rev3 = rev[:].unsqueeze(1).broadcast_to([P, NC, E])
                nxt = not isinstance(n, int) or n + 1 < N
                link(nc.vector.tensor_reduce(top1[:], LG[:], AX.X, ALU.max))
                link(nc.vector.tensor_tensor(CAND[:], LG[:], per_token(top1[:], E), ALU.is_equal))
                link(nc.vector.tensor_tensor(CAND[:], CAND[:], rev3, ALU.mult))
                link(nc.vector.tensor_reduce(cmax[:], CAND[:], AX.X, ALU.max))
                link(nc.vector.tensor_tensor(SEL1[:], CAND[:], per_token(cmax[:], E), ALU.is_equal))
                link(nc.vector.scalar_tensor_tensor(out=LG[:], in0=SEL1[:], scalar=-3e38, in1=LG[:], op0=ALU.mult,
                                                    op1=ALU.add))
                link(nc.vector.tensor_reduce(top2[:], LG[:], AX.X, ALU.max))
                nc.vector.tensor_tensor(gap[:], top2[:], top1[:], ALU.subtract).then_inc(gap_ready, 1)
                mark(nc.vector.tensor_tensor(CAND[:], LG[:], per_token(top2[:], E), ALU.is_equal))
                if nxt:
                    invert(n + 1, 0)
                settled()
                mark(nc.vector.tensor_tensor(CAND[:], CAND[:], rev3, ALU.mult))
                if nxt:
                    divide(n + 1, (c + 1) % TURN, 0)
                settled()
                mark(nc.vector.tensor_reduce(cmax[:], CAND[:], AX.X, ALU.max))
                if nxt:
                    invert(n + 1, 1)
                settled()
                mark(nc.vector.tensor_tensor(SEL2[:], CAND[:], per_token(cmax[:], E), ALU.is_equal))
                if nxt:
                    divide(n + 1, (c + 1) % TURN, 1)
                dve.wait_ge(gap_exp, n + 1)
                link(nc.vector.tensor_scalar(g1[:], g2[:], 1.0, None, ALU.add))
                link(nc.vector.reciprocal(g1[:], g1[:]))
                mark(nc.vector.tensor_tensor(g2[:], g2[:], g1[:], ALU.mult))
                mark(nc.vector.tensor_tensor(SEL1[:], SEL1[:], per_token(g1[:], E), ALU.mult))
                settled()
                link(nc.vector.tensor_tensor(SEL2[:], SEL2[:], per_token(g2[:], E), ALU.mult))
                link(nc.vector.tensor_tensor(WT[:, b], SEL1[:], SEL2[:], ALU.add))
                assert done[0] == (ORDER_F if nxt else ORDER_F - 2), done[0]

            for t in (wv, wv0, wz, wz0):
                last = nc.vector.memset(t[:], 0.0)
            nc.vector.memset(SUMS[:, :, T:TP], 1.0)
            last = nc.vector.memset(rl[:], 0.0)
            last.then_inc(w_zero, 1)
            dve.wait_ge(w_zero, 1)
            dve.wait_ge(w_in, 16 * NW)
            link(nc.vector.tensor_tensor(wv[:], wv[:], wv0[:], ALU.subtract))
            link(nc.vector.tensor_tensor(wz[:], wz[:], wz0[:], ALU.subtract))
            for s in range(G):
                nc.vector.memset(wv[C * s:C * s + 1, C:C + 1], 1.0)
            link(nc.vector.tensor_copy(wz16[:], wz[:]))
            nc.vector.tensor_tensor(wz16[P // 2:P], wz[P // 2:P], wz16[P // 2:P], ALU.subtract).then_inc(w_ready, 1)
            for h in range(2):
                invert(0, h)
                settled()
                divide(0, 0, h)
            start = done[0]
            steps(dve, step)


def layouts(i):
    w8, w7 = i["L0_conv_w8"][:, 0], i["L0_conv_w7"][:, 0, 0]
    p6, p9 = i["L0_conv_p6w"][0, :, :, 0], i["L0_conv_p9w"][0, 0]
    right, left = slice(G - 1, 2 * G - 1), slice(0, G)
    return {
        "ident": np.eye(P, dtype=np.float32),
        "ident16": np.eye(P, dtype=np.float16),
        "eye4": np.tile(np.eye(C, dtype=np.float32), (G, 1)),
        "rev": np.tile(np.arange(E, 0, -1, dtype=np.float32), (P, 1)),
        "w8s": w8[:, :, 0:G].transpose(2, 0, 1).reshape(P, 5),
        "w8e": np.tile(w8[:, :, G], (G, 1)),
        "w7e": np.tile(w7, (G, 1)),
        "p6": np.stack([p6[:, right].T.reshape(P), p6[:, left].T.reshape(P)], 1),
        "p9": np.concatenate([np.repeat(p9[right], C, 0), np.repeat(p9[left], C, 0)], 1),
        "w2t": i["L0_conv_w2"][:, :, 0].transpose(2, 1, 0),
        "wqk": np.concatenate([i["L1_attn_Wq"], i["L1_attn_Wk"]], 1),
        "bqk": np.concatenate([i["L1_attn_bq"], i["L1_attn_bk"]])[None],
        "Wv": i["L1_attn_Wv"],
        "bv": i["L1_attn_bv"][None],
        "wz": np.concatenate([i["L1_ffn_expert_w"].transpose(1, 0, 2).reshape(C, E * C), i["L1_ffn_router_w"]], 1),
        "bz": np.concatenate([i["L1_ffn_expert_b"].reshape(E * C), i["L1_ffn_router_b"]])[None],
    }


def kernel(**inputs):
    import concourse.bacc as bacc
    from concourse.bass_utils import run_bass_kernel_spmd

    nc = bacc.Bacc("TRN2", target_bir_lowering=False, num_devices=1)
    inputs = {n: np.asarray(a) for n, a in inputs.items()}
    arrays = {"x": inputs["x"], **layouts(inputs)}
    arrays = {n: np.ascontiguousarray(a) for n, a in arrays.items()}
    aps = {n: nc.dram_tensor(n, a.shape, mybir.dt.from_np(a.dtype), kind="ExternalInput").ap()
           for n, a in arrays.items()}
    out = nc.dram_tensor("out", (N, C, H, W), F32, kind="ExternalOutput").ap()
    build_program(nc, aps.pop("x"), aps, out)
    r = run_bass_kernel_spmd(nc, [arrays], core_ids=[0])
    return r.results[0]["out"]
```

```python
import math
from contextlib import ExitStack
from typing import NamedTuple

import numpy as np
import concourse.bass as bass
from concourse import mybir

F32 = mybir.dt.float32
F16 = mybir.dt.float16
ALU = mybir.AluOpType
ACT = mybir.ActivationFunctionType
AX = mybir.AxisListType

N, C, H, W = 16, 32, 56, 56
P = 128
G = P // C
NG = N // G
T = H * W
TILE = 448
NT = T // TILE
TR = TILE // W
NC = -(-T // P)
LAST = T - (NC - 1) * P
NP = NC // 2
E = 8
GN_EPS, LN_EPS = 1e-5, 1e-5

XW, XTOP, XLEFT = W + 6, 4, 6
XLEN = (H + 2 * XTOP) * XW + 12
XS_LEN = XLEN - 2 * (G - 1)
YW, YTOP, YLEFT = W + 4, 3, 2
YLEN = (H + 2 * YTOP) * YW + 8
YS_LEN = (H + YTOP) * YW + 4
GR = 2 * XW
ORDER_0, ORDER = 15, 55
ORDER_F = 29


class Places(NamedTuple):
    TK: object
    XH: object
    Y16: object
    US: object
    SQ: object
    KS: object


def newton_rsqrt(link, eng, r, v, t):
    link(eng.tensor_tensor(t, r, r, ALU.mult))
    link(eng.tensor_tensor(t, t, v, ALU.mult))
    link(eng.tensor_scalar(t, t, -0.5, 1.5, ALU.mult, ALU.add))
    return link(eng.tensor_tensor(r, r, t, ALU.mult))


def build_program(nc, x, wts, out):
    def scratch(name, shape, dt):
        return nc.dram_tensor(name, shape, dt, kind="Internal").ap()

    scr = {
        "res": scratch("residual", (N, P, NC * C), F32),
        "val": scratch("values", (N, P, NC * C), F32),
        "ks": scratch("key_stacks", (N, P, T), F16),
        "us": scratch("query_stacks", (N, P, T), F16),
        "sums": scratch("sums", (N, P, T), F32),
        "tokens": scratch("tokens", (N, P, NC * C), F32),
        "ident": wts["ident"],
    }
    prepare(nc, x, wts, scr)
    attend(nc, scr)
    finish(nc, wts, scr, out)


def prepare(nc, x, wts, scr):
    with ExitStack() as ctx:
        def sb(name, shape, dt=F32):
            return ctx.enter_context(nc.sbuf_tensor("sb_" + name, shape, dt))

        def ps(name, shape, dt=F32):
            return ctx.enter_context(nc.psum_tensor(name, shape, dt))

        def sem(name):
            return ctx.enter_context(nc.semaphore(name))

        ident = sb("ident", [P, P])
        ident16 = sb("ident16", [P, P], F16)
        eye4 = sb("eye4", [P, C])
        w8s = sb("w8s", [P, 5])
        w8e = sb("w8e", [P, 5])
        w7e = sb("w7e", [P, 5])
        p6 = sb("p6", [P, 2])
        p9 = sb("p9", [P, 2, C])
        lhs8 = sb("lhs8", [P, 5, C])
        lhs2 = sb("lhs2", [P, 2, C])
        p69 = sb("p69", [P, 2, C])
        wqk = sb("wqk", [C, 2, C])
        wqk0 = sb("wqk0", [C, 2, C])
        wqkT = sb("wqkT", [C, 2, C])
        wqkT4 = sb("wqkT4", [C, 2, G, C])
        mfull = sb("mfull", [P, P])
        mstack = sb("mstack", [P, P], F16)
        X1 = sb("X1", [P, NC * P])
        Xp = sb("Xp", [P, XLEN])
        T2 = sb("T2", [P, YLEN])
        TT = sb("TT", [P, 2, 4 * G, P])
        stacks = sb("stacks", [P, G * XS_LEN])
        XS = stacks[:].rearrange("p (n l) -> p n l", n=G)
        stacks2 = sb("stacks2", [P, G * YS_LEN])
        T2S = stacks2[:].rearrange("p (n l) -> p n l", n=G)
        XI = T2[:, 0:T]
        TM = stacks2[:, 0:G * NC * C]
        def token_places(tk, xh, yu, ks):
            return Places(tk, xh, yu.rearrange("p (k s c) -> p k s c", k=NC, s=G), yu[:, 0:T],
                          ks[:, 0:2 * NC * C].bitcast(F32).rearrange("p (k c) -> p k c", c=C), ks)

        TK, XH = sb("TK", [P, NC, C]), sb("XH", [P, NC, C])
        YU, KS = sb("YU", [P, NC * P], F16), sb("KS", [P, T], F16)
        first = token_places(TK[:], XH[:], YU[:], KS[:])
        own = [first]
        size = NC * C + NC * P // 2 + T // 2
        for n in range(1, G):
            v = stacks[:, (n - 1) * size:n * size]
            own.append(token_places(TM[:, n * NC * C:(n + 1) * NC * C].rearrange("p (k c) -> p k c", c=C),
                                    v[:, 0:NC * C].rearrange("p (k c) -> p k c", c=C),
                                    v[:, NC * C:NC * C + NC * P // 2].bitcast(F16),
                                    v[:, NC * C + NC * P // 2:size].bitcast(F16)))
        stats = sb("stats", [P, NT, 6])
        mv = sb("mv", [P, 2])
        var, rs, tmp1 = sb("var", [P, 1]), sb("rs", [P, 1]), sb("tmp1", [P, 1])
        gsb, gT = sb("gsb", [P, G * P]), sb("gT", [P, G * P])
        adder = sb("adder", [P, P])
        lhs10 = sb("lhs10", [P, 2, G, C])
        lsum, lvar, lrs, ltmp = (sb(n, [P, NC]) for n in ("lsum", "lvar", "lrs", "ltmp"))

        psA = ps("psA", [P, 2, 512])
        psT = ps("psT", [P, 2, 512])
        psG = ps("psG", [P, 512])
        psQ = ps("psQ", [P, 3, 512])

        names = ("w_in w_zero w_dve w_pe x_in xi_used t2_zero xp_ready xs_in stat_var stat_std conv3_full conv5_full "
                 "q_full t2_ready t2s_in t_full t_free gram_done lhs10_ready x1_ready tok_out tk_in tm_cen tm_sq tm_var "
                 "tm_std taps_done gram_out gram_sum xh_ready y_high res_ready res_out val_ready val_out y16_ready k_full ks_ready ks_out u_hi "
                 "u_ready us_out order")
        (w_in, w_zero, w_dve, w_pe, x_in, xi_used, t2_zero, xp_ready, xs_in, stat_var, stat_std, conv3_full, conv5_full,
         q_full, t2_ready, t2s_in, t_full, t_free, gram_done, lhs10_ready, x1_ready, tok_out, tk_in, tm_cen, tm_sq,
         tm_var, tm_std, taps_done, gram_out, gram_sum, xh_ready, y_high, res_ready, res_out, val_ready, val_out, y16_ready, k_full, ks_ready, ks_out,
         u_hi, u_ready, us_out, order) = map(sem, names.split())
        block = ctx.enter_context(nc.Block())

        x_g = x.rearrange("(g n) c h w -> g (n c) (h w)", n=G)
        tok_g = scr["tokens"].rearrange("(g n) p f -> g p n f", n=G)

        def image(name, r):
            return scr[name][bass.ds(r, 1)].rearrange("a p f -> (a p) f")

        NW = 14
        KSETS = 4
        TSETS = G * NT + NT
        HALVES = (range(0, 4), range(4, NT))

        def steps(eng, step):
            step(0, True, False, True)
            with eng.Fori(0, NG - 2) as i:
                step(i + 1, True, True, True)
            step(NG - 1, True, True, False)
            step(NG, False, True, False)

        def xrows(ap, row, col, rows=TR):
            a = row * XW + col
            return ap[..., a:a + rows * XW].rearrange("p (r w) -> p r w", w=XW)[:, :, 0:W]

        def yrows(ap, row, col, rows=TR):
            a = row * YW + col
            return ap[..., a:a + rows * YW].rearrange("p (r w) -> p r w", w=YW)[:, :, 0:W]

        @block.sync
        def _(sp):
            def load(g):
                sp.dma_start(XI, x_g[bass.ds(g, 1)].rearrange("a p t -> (a p) t")).then_inc(x_in, 16)

            load(0)
            for dst, name in ((ident, "ident"), (ident16, "ident16"), (eye4, "eye4"), (w8s, "w8s"), (w8e, "w8e"),
                              (w7e, "w7e")):
                sp.dma_start(dst[:], wts[name]).then_inc(w_in, 16)
            sp.dma_start(p6[:], wts["p6"]).then_inc(w_in, 16)
            sp.dma_start(p9[:].rearrange("p a c -> p (a c)"), wts["p9"]).then_inc(w_in, 16)
            sp.wait_ge(w_zero, 1)
            sp.dma_start(lhs2[0:C, 0, :], wts["w2t"][0]).then_inc(w_in, 16)
            sp.dma_start(lhs2[C:2 * C, 0, :], wts["w2t"][2]).then_inc(w_in, 16)
            sp.dma_start(lhs2[0:C, 1, :], wts["w2t"][1]).then_inc(w_in, 16)
            sp.dma_start(wqk[1:C, :, :], wts["wqk"][1:C, :].rearrange("p (a c) -> p a c", a=2)).then_inc(w_in, 16)
            sp.dma_start(wqk[0:1, :, :], wts["bqk"].rearrange("p (a c) -> p a c", a=2)).then_inc(w_in, 16)
            sp.dma_start(wqk0[1:C, :, :], wts["wqk"][0:1, :].broadcast_to([C - 1, 2 * C]).rearrange(
                "p (a c) -> p a c", a=2)).then_inc(w_in, 16)

            def load_tokens(r):
                sp.dma_start(TK[:].rearrange("p k c -> p (k c)"), image("tokens", r)).then_inc(tk_in, 16)

            def store(m, n, z=first, alone=False):
                r = m * G + n
                sp.wait_ge(res_ready, r + 1)
                sp.dma_start(image("res", r), z.TK.rearrange("p k c -> p (k c)")).then_inc(res_out, 16)
                sp.wait_ge(val_ready, r + 1)
                sp.dma_start(image("val", r), z.XH.rearrange("p k c -> p (k c)")).then_inc(val_out, 16)
                if n + 1 < G and not alone:
                    if n == 0:
                        sp.wait_ge(tok_out, m * 16 + 16)
                    sp.wait_ge(res_out, m * G * 16 + (n + 1) * 16)
                    load_tokens(r + 1)
                sp.wait_ge(ks_ready, m * G * KSETS + (n + 1) * KSETS)
                sp.dma_start(image("ks", r), z.KS).then_inc(ks_out, 16)
                sp.wait_ge(u_ready, m * G * NT + (n + 1) * NT)
                sp.dma_start(image("us", r), z.US).then_inc(us_out, 16)

            def step(g, new, old, more):
                m = g - 1
                if new:
                    sp.wait_ge(xp_ready, g + 1)
                    if old:
                        sp.wait_ge(conv5_full, g * NT)
                    for n in range(G):
                        for s in range(G):
                            sp.dma_start(XS[C * s:C * s + C, n, :],
                                         Xp[C * n:C * n + C, 2 * s:2 * s + XS_LEN]).then_inc(xs_in, 16)
                if old and not new:
                    for n in range(G):
                        store(m, n, own[n], True)
                    return
                if old:
                    store(m, 0)
                if new:
                    sp.wait_ge(t2_ready, g * NT + NT)
                    if old:
                        sp.wait_ge(tok_out, m * 16 + 16)
                    for n in range(G):
                        for s in range(G):
                            sp.dma_start(T2S[C * s:C * s + C, n, :],
                                         T2[C * n:C * n + C, YW * s:YW * s + YS_LEN]).then_inc(t2s_in, 16)
                if old:
                    store(m, 1)
                    store(m, 2)
                if more:
                    sp.wait_ge(taps_done, g + 1)
                    sp.wait_ge(t2s_in, g * 16 * G * G + 16 * G * G)
                    load(g + 1)
                if old:
                    store(m, 3)

            steps(sp, step)
            for done in (res_out, val_out, ks_out, us_out):
                sp.wait_ge(done, N * 16)

        @block.tensor
        def _(pe):
            def conv3(g, i):
                if i >= 2:
                    pe.wait_ge(t2_ready, g * NT + i - 1)
                for j in range(2):
                    for n in range(G):
                        last = nc.tensor.matmul(psA[C * n:C * n + C, i % 2, 0:TILE], lhs2[:, j, :],
                                                xrows(XS[:, n], XTOP + TR * i, XLEFT - 1 + j),
                                                start=(j == 0), stop=(j == 1))
                last.then_inc(conv3_full, 1)

            def turn_stack(g, n, h):
                for k in HALVES[h]:
                    u = n * NT + k
                    if u >= 2:
                        pe.wait_ge(t_free, g * TSETS + u - 1)
                    for q in range(G):
                        a = (XTOP + 2 * (G * k + q)) * XW
                        last = nc.tensor.transpose(psT[0:GR, u % 2, q * P:(q + 1) * P], XS[:, n, a:a + GR], ident[:])
                    last.then_inc(t_full, 1)

            def correlate(g, n, h, beside=()):
                pe.wait_ge(t_free, g * TSETS + n * NT + HALVES[h][-1] + 1)
                for i in range(G * len(HALVES[h])):
                    q = i % G
                    last = nc.tensor.matmul(psG[C * q:C * q + C, n * P:(n + 1) * P], TT[0:GR, h, i, 0:C],
                                            TT[0:GR, h, i, :], start=(h == 0 and i < G),
                                            stop=(h == 1 and i >= G * (len(HALVES[h]) - 1)))
                    if i == G * len(HALVES[h]) - 1:
                        last.then_inc(gram_done, 1)
                    if i % G == G - 1 and i // G < len(beside):
                        part, *args = beside[i // G]
                        part(*args)

            def conv5(g, i, beside=()):
                if i >= 2:
                    pe.wait_ge(x1_ready, g * NT + i - 1)
                for j in range(7):
                    for n in range(G):
                        o = psA[C * n:C * n + C, (NT + i) % 2, 0:TILE]
                        if j < 5:
                            w, v = lhs8[:, j, :], xrows(XS[:, n], TR * i + 2 * j, 2)
                        else:
                            w, v = lhs10[:, j - 5, n, :], yrows(T2S[:, n], TR * i + YTOP * (6 - j), YLEFT)
                        last = nc.tensor.matmul(o, w, v, start=(j == 0), stop=(j == 6))
                    if j == 6:
                        last.then_inc(conv5_full, 1)
                    if j < len(beside):
                        part, *args = beside[j]
                        part(*args)

            def turn_output(g):
                pe.wait_ge(x1_ready, g * NT + NT)
                for k in range(NT):
                    u = G * NT + k
                    pe.wait_ge(t_free, g * TSETS + u - 1)
                    for q in range(min(G, NC - G * k)):
                        a = (G * k + q) * P
                        last = nc.tensor.transpose(psT[:, u % 2, q * P:(q + 1) * P], X1[:, a:a + P], ident[:])
                    last.then_inc(t_full, 1)

            def turn_keys(m, n, s, z=first):
                if s == 0:
                    pe.wait_ge(y16_ready, m * G + n + 1)
                if s == 0 and z is not first:
                    pe.wait_ge(u_ready, (m * G + n) * NT)
                if s == 3:
                    pe.wait_ge(ks_ready, (m * G + n) * KSETS + 1)
                o = psQ[:, s % 3].bitcast(F16)
                for q in range(min(8, NC - 8 * s)):
                    last = nc.tensor.transpose(o[:, q * P:(q + 1) * P], z.Y16[:, 8 * s + q].rearrange("p s c -> p (s c)"),
                                               ident16[:])
                last.then_inc(k_full, 1)

            def queries(m, n, i, z=first):
                if i == 0:
                    pe.wait_ge(ks_ready, (m * G + n) * KSETS + KSETS)
                elif i >= 3:
                    pe.wait_ge(u_ready, (m * G + n) * NT + i - 2)
                nc.tensor.matmul(psQ[:, (KSETS + i) % 3, 0:TILE], mstack[:], z.KS[:, i * TILE:(i + 1) * TILE],
                                 start=True, stop=True).then_inc(q_full, 1)

            def step(g, new, old, more):
                m = g - 1

                def keys_of(n):
                    return [(turn_keys, m, n, s) for s in range(KSETS)] if old else []

                def queries_of(n):
                    return [(queries, m, n, i) for i in range(NT)] if old else []

                def run(parts):
                    for part, *args in parts:
                        part(*args)

                if not new:
                    for n in range(G):
                        for s in range(KSETS):
                            turn_keys(m, n, s, own[n])
                        for i in range(NT):
                            queries(m, n, i, own[n])
                    return
                run(keys_of(0))
                run(queries_of(0))
                if new:
                    pe.wait_ge(xs_in, g * 16 * G * G + 16 * G * G)
                    for i in range(NT):
                        conv3(g, i)
                    between = {(0, 1): keys_of(1), (1, 0): queries_of(1)[0:4], (1, 1): queries_of(1)[4:7],
                               }
                    turn_stack(g, 0, 0)
                    turn_stack(g, 0, 1)
                    for n in range(G):
                        for h in range(2):
                            part = between.get((n, h), [])
                            inside = len(HALVES[h])
                            correlate(g, n, h, part[0:inside])
                            run(part[inside:])
                            if n + 1 < G:
                                turn_stack(g, n + 1, h)
                    for i in range(2):
                        pe.wait_ge(gram_out, g * 2 + i + 1)
                        nc.tensor.matmul(psT[:, i], adder[:], (gsb, gT)[i][:], start=True, stop=True).then_inc(gram_sum, 1)
                    pe.wait_ge(lhs10_ready, g + 1)
                    pe.wait_ge(t2s_in, g * 16 * G * G + 16 * G * G)
                    between = {0: keys_of(2), 1: queries_of(2), 4: keys_of(3), 5: queries_of(3)}
                    for i in range(NT):
                        conv5(g, i, between.get(i, ()))
                    turn_output(g)

            pe.wait_ge(w_dve, 1)
            nc.tensor.matmul(psG[:, 0:P], wqkT4[:, 0], wqkT4[:, 1], start=True, stop=True).then_inc(w_pe, 1)
            pe.wait_ge(w_dve, 2)
            steps(pe, step)

        @block.scalar
        def _(act):
            def to_t2(g, i):
                act.wait_ge(conv3_full, g * NT + i + 1)
                nc.scalar.activation(yrows(T2[:], YTOP + TR * i, YLEFT),
                                     psA[:, i % 2, 0:TILE].rearrange("p (r w) -> p r w", w=W),
                                     ACT.Copy).then_inc(t2_ready, 1)

            def turned(g, n, h):
                if n >= 1:
                    act.wait_ge(gram_done, g * 2 * G + 2 * n + h - 1)
                for k in HALVES[h]:
                    u = n * NT + k
                    a = G * (k - HALVES[h][0])
                    act.wait_ge(t_full, g * TSETS + u + 1)
                    nc.scalar.activation(TT[0:GR, h, a:a + G, :], psT[0:GR, u % 2].rearrange("p (q s) -> p q s", q=G),
                                         ACT.Copy).then_inc(t_free, 1)

            def squares(m, n, z=first):
                if n >= 1 and z is first:
                    act.wait_ge(ks_out, m * G * 16 + n * 16)
                act.wait_ge(tm_cen, m * G + n + 1)
                nc.scalar.activation(z.SQ, z.XH, ACT.Square).then_inc(tm_sq, 1)
                act.wait_ge(tm_var, m * G + n + 1)
                nc.scalar.activation(lrs[:], lvar[:], ACT.Sqrt).then_inc(tm_std, 1)

            def high_parts(m, n, z=first):
                if n >= 1 and z is first:
                    act.wait_ge(us_out, m * G * 16 + n * 16)
                act.wait_ge(xh_ready, m * G + n + 1)
                for s in (0, 2):
                    nc.scalar.activation(z.Y16[:, :, s, :], z.XH, ACT.Copy).then_inc(y_high, 1)

            def keys(m, n, z=first):
                for s in range(KSETS):
                    a = 8 * s * P
                    w = min(8 * P, T - a)
                    act.wait_ge(k_full, (m * G + n) * KSETS + s + 1)
                    nc.scalar.activation(z.KS[:, a:a + w], psQ[:, s % 3].bitcast(F16)[:, 0:w], ACT.Copy).then_inc(ks_ready, 1)

            def query_high(m, n, tiles=range(NT), z=first):
                for i in tiles:
                    act.wait_ge(q_full, (m * G + n) * NT + i + 1)
                    nc.scalar.activation(z.US[:, i * TILE:(i + 1) * TILE], psQ[:, (KSETS + i) % 3, 0:TILE],
                                         ACT.Copy).then_inc(u_hi, 1)

            def step(g, new, old, more):
                m = g - 1
                if old and not new:
                    for n in range(G + 1):
                        if n < G:
                            squares(m, n, own[n])
                        if n >= 1:
                            keys(m, n - 1, own[n - 1])
                        if n < G:
                            high_parts(m, n, own[n])
                        if n >= 1:
                            query_high(m, n - 1, z=own[n - 1])
                    return
                if old:
                    act.wait_ge(t_free, g * TSETS)
                    act.dma_start(tok_g[bass.ds(m, 1), :, 1:G].rearrange("a p n f -> (a p) n f"),
                                  TM.rearrange("p (n f) -> p n f", n=G)[:, 1:G]).then_inc(tok_out, 16)
                    squares(m, 0)
                    high_parts(m, 0)
                    keys(m, 0)
                    query_high(m, 0)
                if new:
                    act.wait_ge(t2_zero, g + 1)
                    for i in range(NT):
                        to_t2(g, i)
                if new:
                    turned(g, 0, 0)
                    turned(g, 0, 1)
                if old:
                    squares(m, 1)
                if new:
                    turned(g, 1, 0)
                if old:
                    high_parts(m, 1)
                if old:
                    keys(m, 1)
                if new:
                    turned(g, 1, 1)
                if old:
                    query_high(m, 1, range(0, 4))
                if new:
                    turned(g, 2, 0)
                if old:
                    query_high(m, 1, range(4, NT))
                if new:
                    turned(g, 2, 1)
                if old:
                    squares(m, 2)
                if new:
                    turned(g, 3, 0)
                    turned(g, 3, 1)
                if old:
                    high_parts(m, 2)
                    keys(m, 2)
                    query_high(m, 2)
                    squares(m, 3)
                    high_parts(m, 3)
                    keys(m, 3)
                if more:
                    act.wait_ge(stat_var, g + 2)
                    nc.scalar.activation(rs[:], var[:], ACT.Sqrt).then_inc(stat_std, 1)
                if old:
                    query_high(m, 3)
                    act.wait_ge(res_out, m * G * 16 + G * 16)
                if new:
                    act.wait_ge(conv5_full, g * NT + NT)
                    tm4 = TM.rearrange("p (n k c) -> p n k c", n=G, k=NC)
                    for k in range(NT):
                        u = G * NT + k
                        q = min(G, NC - G * k)
                        act.wait_ge(t_full, g * TSETS + u + 1)
                        v = psT[:, u % 2, 0:q * P].rearrange("p (q n c) -> p n q c", n=G, c=C)
                        nc.scalar.activation(TK[:, G * k:G * k + q, :], v[:, 0], ACT.Copy)
                        nc.scalar.activation(tm4[:, 1:G, G * k:G * k + q, :], v[:, 1:G], ACT.Copy).then_inc(t_free, 1)
                if old:
                    act.wait_ge(ks_out, m * G * 16 + G * 16)
                    act.wait_ge(us_out, m * G * 16 + G * 16)

            act.wait_ge(stat_var, 1)
            nc.scalar.activation(rs[:], var[:], ACT.Sqrt).then_inc(stat_std, 1)
            steps(act, step)

        @block.gpsimd
        def _(pool):
            def step(g, new, old, more):
                if old:
                    for n in range(G):
                        pool.wait_ge(xh_ready, (g - 1) * G + n + 1)
                        z = first if new else own[n]
                        nc.gpsimd.tensor_tensor(z.TK, z.TK, z.XH, ALU.add).then_inc(res_ready, 1)

            steps(pool, step)

        @block.vector
        def _(dve):
            done = [0]
            base = [0]

            def mark(ins):
                done[0] += 1
                return ins.then_inc(order, 1)

            def settled():
                dve.wait_ge(order, base[0] + done[0])

            def link(ins):
                mark(ins)
                settled()

            nc.vector.memset(lhs2[:], 0.0)
            nc.vector.memset(wqk[:], 0.0)
            nc.vector.memset(wqk0[:], 0.0).then_inc(w_zero, 1)
            nc.vector.memset(Xp[:], 0.0)
            nc.vector.memset(X1[:, T:NC * P], 0.0)
            nc.vector.memset(lhs10[:], 0.0).then_inc(w_zero, 1)
            dve.wait_ge(w_zero, 2)
            dve.wait_ge(w_in, 16 * NW)
            for s in range(G):
                nc.vector.tensor_copy(adder[:, C * s:C * s + C], eye4[:])
            for i in range(5):
                nc.vector.tensor_scalar(lhs8[:, i, :], eye4[:], w8s[:, i:i + 1], None, ALU.mult)
            for i in range(2):
                link(nc.vector.tensor_scalar(p69[:, i, :], p9[:, i, :], p6[:, i:i + 1],
                                             -1.0 / math.sqrt(H * W * C * 7), ALU.mult, ALU.mult))
            link(nc.vector.tensor_tensor(wqk[:], wqk[:], wqk0[:], ALU.subtract))
            for i in range(2):
                link(nc.vector.transpose(wqkT[:, i, :], wqk[:, i, :]))
            for i in range(2):
                for s in range(G):
                    last = nc.vector.tensor_copy(wqkT4[:, i, s, :], wqkT[:, i, :])
            last.then_inc(w_dve, 1)
            dve.wait_ge(w_pe, 1)
            link(nc.vector.tensor_scalar(mfull[:], psG[:, 0:P], 1.0 / math.sqrt(C), None, ALU.mult))
            link(nc.vector.tensor_copy(mstack[:], mfull[:]))
            link(nc.vector.tensor_tensor(mstack[P // 2:P], mfull[P // 2:P], mstack[P // 2:P], ALU.subtract))
            for s in (1, 3):
                link(nc.vector.memset(mstack[C * s:C * s + 1, :], 0.0))
                link(nc.vector.memset(mstack[:, C * s:C * s + 1], 0.0))
            nc.vector.memset(tmp1[:], 0.0).then_inc(w_dve, 1)

            x3 = X1[:, 0:T].rearrange("p (r w) -> p r w", w=W)
            xi3 = XI.rearrange("p (r w) -> p r w", w=W)

            def statistics(g):
                dve.wait_ge(x_in, g * 16 + 16)
                for i in range(NT):
                    last = nc.vector.bn_stats(stats[:, i, :], XI[:, i * TILE:(i + 1) * TILE])
                link(last)
                nc.vector.memset(tmp1[:], 0.0)
                link(nc.vector.bn_aggr(mv[:], stats[:].rearrange("p a b -> p (a b)")))
                nc.vector.tensor_scalar(var[:], mv[:, 1:2], GN_EPS, None, ALU.add).then_inc(stat_var, 1)

            def normalise(g):
                dve.wait_ge(stat_std, g + 1)
                link(nc.vector.reciprocal(rs[:], rs[:]))
                newton_rsqrt(link, nc.vector, rs[:], var[:], tmp1[:])
                nc.vector.tensor_scalar(xrows(Xp[:], XTOP, XLEFT, H), xi3, mv[:, 0:1], rs[:],
                                        ALU.subtract, ALU.mult).then_inc(xp_ready, 1)

            def taps5(rows):
                for i in rows:
                    link(nc.vector.scalar_tensor_tensor(out=x3, in0=xrows(Xp[:], 2 * i, 10, H), scalar=w8e[:, i:i + 1],
                                                        in1=x3, op0=ALU.mult, op1=ALU.add))

            def per_token(a):
                return a[:].unsqueeze(2).broadcast_to([P, NC, C])

            def token_norm(m, n, fill, z=first):
                r = m * G + n
                if n == 0 or z is not first:
                    dve.wait_ge(t_free, m * TSETS + TSETS)
                else:
                    dve.wait_ge(tk_in, m * (G - 1) * 16 + n * 16)
                link(nc.vector.tensor_reduce(lsum[:], z.TK, AX.X, ALU.add))
                link(nc.vector.tensor_scalar(lsum[:], lsum[:], 1.0 / C, None, ALU.mult))
                if n >= 1 and z is first:
                    dve.wait_ge(val_out, m * G * 16 + n * 16)
                nc.vector.tensor_tensor(z.XH, z.TK, per_token(lsum), ALU.subtract).then_inc(tm_cen, 1)
                if fill:
                    taps5(fill)
                dve.wait_ge(tm_sq, r + 1)
                link(nc.vector.tensor_reduce(lvar[:], z.SQ, AX.X, ALU.add))
                nc.vector.tensor_scalar(lvar[:], lvar[:], 1.0 / C, LN_EPS, ALU.mult, ALU.add).then_inc(tm_var, 1)
                dve.wait_ge(tm_std, r + 1)
                link(nc.vector.reciprocal(lrs[:], lrs[:]))
                newton_rsqrt(link, nc.vector, lrs[:], lvar[:], ltmp[:])
                nc.vector.tensor_tensor(z.XH, z.XH, per_token(lrs), ALU.mult).then_inc(xh_ready, 1)
                dve.wait_ge(xh_ready, r + 1)
                dve.wait_ge(y_high, r * 2 + 1)
                link(nc.vector.tensor_tensor(z.Y16[:, :, 1, :], z.XH, z.Y16[:, :, 0, :], ALU.subtract))
                link(nc.vector.tensor_copy(z.Y16[:, :, 3, :], z.Y16[:, :, 1, :]))
                dve.wait_ge(y_high, r * 2 + 2)
                nc.vector.memset(z.Y16[:, :, :, 0:1], 1.0).then_inc(y16_ready, 1)
                dve.wait_ge(res_ready, r + 1)
                nc.vector.memset(z.XH[:, :, 0:1], 1.0).then_inc(val_ready, 1)

            def query_low(m, n, z=first):
                for i in range(NT):
                    dve.wait_ge(u_hi, (m * G + n) * NT + i + 1)
                    v = z.US[P // 2:P, i * TILE:(i + 1) * TILE]
                    nc.vector.tensor_tensor(v, psQ[P // 2:P, (KSETS + i) % 3, 0:TILE], v, ALU.subtract).then_inc(u_ready, 1)

            def taps_row(rows):
                for i in rows:
                    last = nc.vector.scalar_tensor_tensor(out=x3, in0=yrows(T2[:], YTOP, i, H), scalar=w7e[:, i:i + 1],
                                                          in1=x3, op0=ALU.mult, op1=ALU.add)
                    if i < 4:
                        link(last)
                    else:
                        last.then_inc(taps_done, 1)

            def mixing(g):
                dve.wait_ge(gram_done, g * 2 * G + 2 * G)
                nc.vector.tensor_copy(gsb[:], psG[:]).then_inc(gram_out, 1)
                dve.wait_ge(gram_out, g * 2 + 1)
                nc.vector.transpose(gT[:], gsb[:]).then_inc(gram_out, 1)
                dve.wait_ge(gram_sum, g * 2 + 2)
                for s in range(G):
                    for i, t in ((0, s), (1, G - 1 - s)):
                        if i == 0 or s < G - 1:
                            v = psT[C * s:C * s + C, 1 - i].rearrange("p (n s c) -> p s n c", n=G, s=G)[:, t]
                            last = nc.vector.tensor_tensor(lhs10[C * s:C * s + C, i], v, p69[C * s:C * s + C, i].unsqueeze(
                                1).broadcast_to([C, G, C]), ALU.mult)
                last.then_inc(lhs10_ready, 1)

            def step(g, new, old, more):
                m = g - 1
                if old:
                    base[0] = FIRST + (g - 1) * ORDER if new else base[0] + done[0]
                done[0] = 0

                def add(tiles):
                    for i in tiles:
                        dve.wait_ge(conv5_full, g * NT + i + 1)
                        v = X1[:, i * TILE:(i + 1) * TILE]
                        nc.vector.tensor_tensor(v, psA[:, (NT + i) % 2, 0:TILE], v, ALU.add).then_inc(x1_ready, 1)

                if old and not new:
                    for n in range(G + 1):
                        if n < G:
                            token_norm(m, n, (), own[n])
                        if n >= 1:
                            query_low(m, n - 1, own[n - 1])
                    return
                if old:
                    token_norm(m, 0, ())
                if new:
                    dve.wait_ge(xp_ready, g + 1)
                    if old:
                        dve.wait_ge(t_full, g * TSETS)
                    nc.vector.scalar_tensor_tensor(out=x3, in0=xrows(Xp[:], 0, 10, H), scalar=w8e[:, 0:1], in1=xi3,
                                                   op0=ALU.mult, op1=ALU.add).then_inc(xi_used, 1)
                    dve.wait_ge(xi_used, g + 1)
                    inside, end = YTOP * YW + YLEFT, (YTOP + H - 1) * YW + YLEFT + W
                    nc.vector.memset(T2[:, 0:inside], 0.0)
                    nc.vector.memset(T2[:, inside + W:inside + W + (H - 1) * YW].rearrange(
                        "p (r w) -> p r w", w=YW)[:, :, 0:YW - W], 0.0)
                    nc.vector.memset(T2[:, end:YLEN], 0.0).then_inc(t2_zero, 1)
                if old:
                    query_low(m, 0)
                if new:
                    taps5((1, 2, 3) if old else (1, 2, 3, 4))
                if old:
                    token_norm(m, 1, (4,) if new else ())
                if new:
                    dve.wait_ge(t2_ready, g * NT + NT)
                    taps_row((0, 1))
                if old:
                    query_low(m, 1)
                    token_norm(m, 2, ())
                if new:
                    mixing(g)
                    taps_row((2, 3, 4))
                    dve.wait_ge(taps_done, g + 1)
                    add((0,))
                if old:
                    query_low(m, 2)
                if new:
                    add((1,))
                if old:
                    token_norm(m, 3, ())
                if new:
                    add((2,))
                    if more:
                        statistics(g + 1)
                    add((3,))
                    if more:
                        normalise(g + 1)
                    add((4,))
                if old:
                    query_low(m, 3)
                if new:
                    add((5, 6))
                if old:
                    dve.wait_ge(val_out, m * G * 16 + G * 16)
                if more:
                    assert done[0] == (ORDER if old else ORDER_0), done[0]

            statistics(0)
            normalise(0)
            base[0] = done[0]
            FIRST = done[0] + ORDER_0
            steps(dve, step)


def attend(nc, scr):
    with ExitStack() as ctx:
        def sb(name, shape, dt=F32):
            return ctx.enter_context(nc.sbuf_tensor("at_" + name, shape, dt))

        def ps(name, shape, dt=F32):
            return ctx.enter_context(nc.psum_tensor("at_" + name, shape, dt))

        def sem(name):
            return ctx.enter_context(nc.semaphore("at_" + name))

        TP = NC * P
        NU = NP + 1
        NQ = NC // G
        B = 3
        KS, US = sb("KS", [P, B, TP], F16), sb("US", [P, B, TP], F16)
        V = sb("V", [P, B, NC, C])
        O = sb("O", [P, B, T])
        PR = sb("PR", [P, 4, 2, TILE])
        PL = sb("PL", [P, TILE])
        XM = sb("XM", [P, NT, NC])
        negm = sb("negm", [P, NC])
        mrow = sb("mrow", [NC, 2, P], F16)
        ident = sb("ident", [P, P])
        psS = ps("psS", [P, 2, 2, 512])
        psX = ps("psX", [P, 3, 512])
        psV = ps("psV", [P, 512])

        k_in = [sem(f"k_in{b}") for b in range(B)]
        names = ("c_in zeroed s_full p_ready p_used v_full x_full x_done negm_ready mT_full mrow_ready m_in o_ready order")
        (c_in, zeroed, s_full, p_ready, p_used, v_full, x_full, x_done, negm_ready, mT_full, mrow_ready, m_in, o_ready,
         order) = map(sem, names.split())
        o_out = [sem(f"o_out{b}") for b in range(B)]
        block = ctx.enter_context(nc.Block())
        FREE_X = 4
        FREE = 2
        FREE_V = 1
        FREE_O = 16
        FULL = (N - 1) // B - 1

        def round_of(i, b):
            return i * B + b

        @block.sync
        def _(sp):
            def load(n, b):
                for dst, src in ((KS[:, b, 0:T], "ks"), (US[:, b, 0:T], "us"),
                                 (V[:, b].rearrange("p k c -> p (k c)"), "val")):
                    sp.dma_start(dst, scr[src][bass.ds(n, 1)].rearrange("a p t -> (a p) t")).then_inc(k_in[b], 16)

            def max_rows(n, b):
                sp.wait_ge(mrow_ready, n + 1)
                for h in range(2):
                    row = C * (2 * h + 1)
                    sp.dma_start(US[row:row + 1, b, :].rearrange("a (k c) -> a k c", k=NC),
                                 mrow[:, h, :]).then_inc(m_in, 16)

            def store(n, b):
                sp.wait_ge(o_ready, n * NT + NT + FREE_V)
                sp.dma_start(scr["sums"][bass.ds(n, 1)].rearrange("a p t -> (a p) t"), O[:, b]).then_inc(o_out[b], 16)

            sp.dma_start(ident[:], scr["ident"]).then_inc(c_in, 16)
            sp.wait_ge(zeroed, 1)
            for b in range(B):
                load(b, b)
            max_rows(0, 0)

            def step(n, b, more, last=False):
                if not last:
                    max_rows(n + 1, (b + 1) % B)
                store(n, b)
                if more:
                    sp.wait_ge(v_full, (n + 1) * NT)
                    load(n + B, b)

            with sp.Fori(0, FULL) as i:
                for b in range(B):
                    step(round_of(i, b), b, True)
            for n in range(FULL * B, N):
                step(n, n % B, n + B < N, n == N - 1)
            for b in range(B):
                sp.wait_ge(o_out[b], 16 * len(range(b, N, B)) + FREE_O)

        @block.tensor
        def _(pe):
            def scores(n, b, t, u):
                base = (n * NT + t) * NU
                if u == 0:
                    pe.wait_ge(p_ready, base)
                elif u >= 2:
                    pe.wait_ge(p_ready, base + u - 1)
                chunks = (2 * u, 2 * u + 1) if u < NP else (2 * u,)
                for j, c in enumerate(chunks):
                    last = nc.tensor.matmul(psS[:, u % 2, j, 0:TILE], KS[:, b, c * P:(c + 1) * P],
                                            US[:, b, bass.ts(t, TILE)], start=True, stop=True)
                last.then_inc(s_full, 1)

            def maxima(n, b, t, c):
                base = (n * NT + t) * NC + FREE_X
                bank = 1 if c == NC - 1 else c % 3
                if c == NC - 1:
                    pe.wait_ge(x_done, base + c - 1)
                elif c == 1:
                    pe.wait_ge(x_done, base)
                else:
                    pe.wait_ge(x_done, base + c - 2 - (c == 0))
                nc.tensor.matmul(psX[:, bank, 0:TILE], US[:, b, c * P:(c + 1) * P], KS[:, b, bass.ts(t, TILE)],
                                 start=True, stop=True).then_inc(x_full, 1)

            def turn_max(n):
                pe.wait_ge(negm_ready, n + 1)
                nc.tensor.transpose(psX[0:NC, 1, 0:P], negm[:], ident[:]).then_inc(mT_full, 1)

            def sums(n, b, t, k):
                base = (n * NT + t) * NU
                if k == NQ - 1:
                    pe.wait_ge(p_ready, base + 2 * k + 2)
                if k == 0:
                    pe.wait_ge(o_ready, n * NT + t + FREE_V)
                for q in range(G):
                    last = nc.tensor.matmul(psV[C * q:C * q + C, 0:TILE], V[:, b, G * k + q, :],
                                            PR[:, (2 * k + q // 2) % 4, q % 2, :], start=(k == 0), stop=(k == NQ - 1))
                last.then_inc(p_used, 1)

            def last_sums(n, b, t):
                pe.wait_ge(p_ready, (n * NT + t + 1) * NU)
                QW = TILE // G
                for q in range(G):
                    last = nc.tensor.matmul(psV[C * q:C * q + C, q * QW:(q + 1) * QW], V[:, b, NC - 1, :],
                                            PL[:, q * QW:(q + 1) * QW], start=False, stop=True, skip_group_check=True)
                last.then_inc(v_full, 1)

            def tile_body(n, b, t, nxt, mx, turn=False):
                for k in range(NQ):
                    for i in range(G):
                        if i == 1 or (i == 2 and 2 * k + 3 < NU):
                            scores(n, b, t, 2 * k + i + 1)
                        if i == (3 if k < NQ - 1 else 2):
                            sums(n, b, t, k)
                        if k == NQ - 1 and i >= 2 and nxt:
                            if turn and i == 2:
                                pe.wait_ge(m_in, 32 * (n + 2))
                            scores(*nxt, i - 2)
                        if mx:
                            maxima(*mx, G * k + i)
                        if turn and k == 0 and i == 0:
                            turn_max(n + 1)
                            pe.wait_ge(mrow_ready, n + 2)
                last_sums(n, b, t)
                if mx:
                    maxima(*mx, NC - 1)

            def step(n, b, ahead):
                b1, b2 = (b + 1) % B, (b + 2) % B
                with pe.Fori(0, NT - 1) as t:
                    tile_body(n, b, t, (n, b, t + 1), (n + 1, b1, t + 1) if ahead >= 1 else None)
                if ahead >= 2:
                    pe.wait_ge(k_in[b2], 48 * loads(n, 2))
                tile_body(n, b, NT - 1, (n + 1, b1, 0) if ahead >= 1 else None,
                          (n + 2, b2, 0) if ahead >= 2 else None, turn=ahead >= 1)

            def loads(n, d):
                if isinstance(n, int):
                    return (n + d) // B + 1
                i, b = now
                return i + (b + d) // B + 1

            pe.wait_ge(c_in, 16)
            pe.wait_ge(zeroed, 1)
            pe.wait_ge(k_in[0], 48)
            with pe.Fori(0, NT) as t:
                for c in range(NC):
                    maxima(0, 0, t, c)
            turn_max(0)
            pe.wait_ge(k_in[1], 48)
            pe.wait_ge(mrow_ready, 1)
            for c in range(NC):
                maxima(1, 1, 0, c)
            pe.wait_ge(m_in, 32)
            scores(0, 0, 0, 0)
            scores(0, 0, 0, 1)
            with pe.Fori(0, FULL) as i:
                for b in range(B):
                    now = (i, b)
                    step(round_of(i, b), b, 2)
            for n in range(FULL * B, N):
                step(n, n % B, N - 1 - n)

        @block.scalar
        def _(act):
            def exponentials(base, j, u):
                act.wait_ge(s_full, base + u + 1)
                if u < NP:
                    if u % 2 == 0:
                        act.wait_ge(p_used, j * NQ + u // 2 - 1 + FREE)
                    nc.scalar.activation(PR[:, u % 4], psS[:, u % 2, :, 0:TILE], ACT.Exp).then_inc(p_ready, 1)
                else:
                    nc.scalar.activation(PL[0:LAST], psS[0:LAST, u % 2, 0, 0:TILE], ACT.Exp).then_inc(p_ready, 1)

            def tile_body(n, b, t, more=True):
                j = n * NT + t
                base = j * NU
                for u in range(2, NU):
                    exponentials(base, j, u)
                if more:
                    for u in range(2):
                        exponentials(base + NU, j + 1, u)
                act.wait_ge(v_full, j + 1)
                nc.scalar.activation(O[:, b, bass.ts(t, TILE)], psV[:, 0:TILE], ACT.Copy).then_inc(o_ready, 1)

            act.wait_ge(zeroed, 1)
            for u in range(2):
                exponentials(0, 0, u)
            with act.Fori(0, FULL) as i:
                for b in range(B):
                    act.wait_ge(o_out[b], i * 16 + FREE_O)
                    with act.Fori(0, NT) as t:
                        tile_body(round_of(i, b), b, t)
            for n in range(FULL * B, N):
                act.wait_ge(o_out[n % B], n // B * 16 + FREE_O)
                with act.Fori(0, NT - 1) as t:
                    tile_body(n, n % B, t)
                tile_body(n, n % B, NT - 1, n < N - 1)

        @block.vector
        def _(dve):
            def maxima(n, t):
                base = (n * NT + t) * NC
                for c in range(NC):
                    bank = 1 if c == NC - 1 else c % 3
                    dve.wait_ge(x_full, base + c + 1)
                    nc.vector.tensor_reduce(XM[:, bass.ds(t, 1), c:c + 1], psX[:, bank, 0:TILE].unsqueeze(1),
                                            AX.X, ALU.max).then_inc(x_done, 1)

            def max_parts(n):
                dve.wait_ge(x_done, (n * NT + NT) * NC + FREE_X)
                nc.vector.tensor_reduce(negm[:], XM[:].rearrange("p t c -> p c t"), AX.X, ALU.max,
                                        negate=True).then_inc(negm_ready, 1)

            def max_halves(n):
                dve.wait_ge(mT_full, n + 1)
                dve.wait_ge(m_in, 32 * n)
                nc.vector.tensor_copy(mrow[:, 0, :], psX[0:NC, 1, 0:P]).then_inc(order, 1)
                dve.wait_ge(order, n + 1)
                nc.vector.tensor_tensor(mrow[:, 1, :], psX[0:NC, 1, 0:P], mrow[:, 0, :],
                                        ALU.subtract).then_inc(mrow_ready, 1)

            def first_maxima(n, ahead, turned):
                dve.wait_ge(negm_ready, n)
                for c in range(NC):
                    bank = 1 if c == NC - 1 else c % 3
                    dve.wait_ge(x_full, n * NT * NC + c + 1)
                    nc.vector.tensor_reduce(XM[:, 0:1, c:c + 1], psX[:, bank, 0:TILE].unsqueeze(1),
                                            AX.X, ALU.max).then_inc(x_done, 1)
                    if c == 0 and turned is not None:
                        max_halves(turned)

            def step(n, ahead):
                if ahead >= 1:
                    with dve.Fori(0, NT - 1) as t:
                        maxima(n + 1, t + 1)
                    max_parts(n + 1)
                if ahead >= 2:
                    first_maxima(n + 2, ahead, n + 1)
                elif ahead == 1:
                    max_halves(n + 1)

            nc.vector.memset(XM[:], 0.0).then_inc(x_done, FREE_X)
            nc.vector.memset(PL[:], 0.0).then_inc(p_used, FREE)
            for b in range(B):
                nc.vector.memset(KS[:, b, T:TP], 0.0).then_inc(o_out[b], FREE_O)
            nc.vector.memset(US[:, 0, T:TP], 0.0).then_inc(o_ready, FREE_V)
            nc.vector.memset(US[:, 1:B, T:TP], 0.0).then_inc(zeroed, 1)
            with dve.Fori(0, NT) as t:
                maxima(0, t)
            max_parts(0)
            max_halves(0)
            first_maxima(1, 2, None)
            with dve.Fori(0, FULL) as i:
                for b in range(B):
                    step(round_of(i, b), 2)
            for n in range(FULL * B, N):
                step(n, N - 1 - n)
def finish(nc, wts, scr, out):
    with ExitStack() as ctx:
        def sb(name, shape, dt=F32):
            return ctx.enter_context(nc.sbuf_tensor("fi_" + name, shape, dt))

        def ps(name, shape, dt=F32):
            return ctx.enter_context(nc.psum_tensor("fi_" + name, shape, dt))

        def sem(name):
            return ctx.enter_context(nc.semaphore("fi_" + name))

        TP = NC * P
        NU = NP + 1
        KSETS = 4
        QSETS = -(-NC // G)
        EC = E * C
        WZ = EC + E
        ident, ident16 = sb("ident", [P, P]), sb("ident16", [P, P], F16)
        wv, wv0 = sb("wv", [P, C + 1]), sb("wv0", [P, C + 1])
        wz, wz0 = sb("wz", [P, WZ]), sb("wz0", [P, WZ])
        wz16 = sb("wz16", [P, WZ], F16)
        rev = sb("rev", [P, E])
        SUMS = sb("SUMS", [P, 2, TP])
        RES = sb("RES", [P, 2, NC, C])
        ZS = sb("ZS", [P, 2, TP], F16)
        WT = sb("WT", [P, 2, NC, E])
        OUT = sb("OUT", [P, 2, QSETS * P])
        T1 = sb("T1", [P, 4, NC, C])
        rl = sb("rl", [P, 2, NP + 1])
        XH, SQ = sb("XH", [P, NC, C]), sb("SQ", [P, NC, C])
        lsum, lvar, lrs, ltmp = (sb(n, [P, NC]) for n in ("lsum", "lvar", "lrs", "ltmp"))
        Z16 = sb("Z16", [P, NC, G, C], F16)
        LG, CAND, SEL1, SEL2 = (sb(n, [P, NC, E]) for n in ("LG", "CAND", "SEL1", "SEL2"))
        top1, top2, cmax, gap, g1, g2 = (sb(n, [P, NC]) for n in ("top1", "top2", "cmax", "gap", "g1", "g2"))
        WE = sb("WE", [P, QSETS, E, G, C])
        psO = ps("psO", [P, 2, 512])
        psK = ps("psK", [P, 2, 1024], F16)
        psE = ps("psE", [P, 2, 512])
        psB = ps("psB", [P, 2, 512])
        psL = psB[:, 1, 0:NC * E]

        names = ("w_in w_zero w_ready o_full o_done t1_ready t1_cen t1_sq t1_var t1_std xh_ready z_high z16_ready k_full zs_ready "
                 "l_full lg_ready gap_ready gap_exp gates_ready e_full we_ready half_folded folded set_done out_ready order")
        (w_in, w_zero, w_ready, o_full, o_done, t1_ready, t1_cen, t1_sq, t1_var, t1_std, xh_ready, z_high, z16_ready, k_full, zs_ready,
         l_full, lg_ready, gap_ready, gap_exp, gates_ready, e_full, we_ready, half_folded, folded, set_done, out_ready,
         order) = map(sem, names.split())
        sums_in, res_in, out_done = ([sem(f"{s}{b}") for b in range(2)] for s in ("sums_in", "res_in", "out_done"))
        block = ctx.enter_context(nc.Block())
        NW = 3 + 6 * G
        STORES = 16 * (G + 1)
        FREE_OUT = 16
        FIRST, TURN = 3, 4
        assert N % TURN == 0

        def steps(eng, step):
            for n in range(FIRST):
                step(n, n % TURN, n // 2)
            with eng.Fori(0, (N - TURN) // TURN) as i:
                for n in range(FIRST, FIRST + TURN):
                    step(i * TURN + n, n % TURN, i * 2 + n // 2)
            for n in range(N - 1, N + 1):
                step(n, n % TURN, n // 2)

        def beyond(n, k):
            return not isinstance(n, int) or n > k

        def load_weights(eng, dst, dst0, w, b, n):
            for s in range(G):
                eng.dma_start(dst[C * s + 1:C * s + C, 0:n], wts[w][1:C, :]).then_inc(w_in, 16)
                eng.dma_start(dst[C * s:C * s + 1, 0:n], wts[b]).then_inc(w_in, 16)
                eng.dma_start(dst0[C * s + 1:C * s + C, 0:n], wts[w][0:1, :].broadcast_to([C - 1, n])).then_inc(w_in, 16)

        @block.sync
        def _(sp):
            def load(n, b):
                if beyond(n, 1):
                    sp.wait_ge(o_full, n * 2 - 2)
                sp.dma_start(SUMS[:, b, 0:T], scr["sums"][bass.ds(n, 1)].rearrange(
                    "a p t -> (a p) t")).then_inc(sums_in[b], 16)
                if beyond(n, 1):
                    sp.wait_ge(t1_ready, n - 1)
                sp.dma_start(RES[:, b].rearrange("p k c -> p (k c)"), scr["res"][bass.ds(n, 1)].rearrange(
                    "a p f -> (a p) f")).then_inc(res_in[b], 16)

            def store(n, b):
                o = out[bass.ds(n, 1)].rearrange("a c h w -> (a c) (h w)")
                full = QSETS - 1
                sp.wait_ge(out_ready, n + 1)
                for q in range(G):
                    sp.dma_start(o[:, 0:full * G * P].rearrange("c (k q p) -> c k q p", q=G, p=P)[:, :, q],
                                 OUT[C * q:C * q + C, b, 0:full * P].rearrange("c (k p) -> c k p", p=P)).then_inc(
                                     out_done[b], 16)
                sp.dma_start(o[:, full * G * P:T], OUT[0:C, b, full * P:full * P + LAST]).then_inc(out_done[b], 16)

            def step(n, c, r):
                b = c % 2
                if not isinstance(n, int) or n + 1 < N:
                    load(n + 1, 1 - b)
                if beyond(n, 1):
                    store(n - 2, b)

            sp.dma_start(ident[:], wts["ident"]).then_inc(w_in, 16)
            sp.dma_start(ident16[:], wts["ident16"]).then_inc(w_in, 16)
            sp.dma_start(rev[:], wts["rev"]).then_inc(w_in, 16)
            load(0, 0)
            sp.wait_ge(w_zero, 1)
            load_weights(sp, wv, wv0, "Wv", "bv", C)
            steps(sp, step)
            store(N - 1, 1)
            for b in range(2):
                sp.wait_ge(out_done[b], STORES * (N // 2) + FREE_OUT)

        @block.tensor
        def _(pe):
            def project(n, b, r, halves):
                for h in halves:
                    if h == 0:
                        pe.wait_ge(sums_in[b], (r + 1) * 16)
                    if beyond(n, 0):
                        pe.wait_ge(o_done, n * 2 + h - 1)
                    for q in range(NP + h):
                        a = (h * NP + q) * P
                        last = nc.tensor.matmul(psO[:, h, q * (C + 1):(q + 1) * (C + 1)], SUMS[:, b, a:a + P],
                                                wv[:], start=True, stop=True)
                    last.then_inc(o_full, 1)

            def turn_tokens(n, s):
                if beyond(n, 0) or s >= 2:
                    pe.wait_ge(zs_ready, n * KSETS + s - 1)
                for q in range(min(8, NC - 8 * s)):
                    last = nc.tensor.transpose(psK[:, s % 2, q * P:(q + 1) * P],
                                               Z16[:, 8 * s + q].rearrange("p s c -> p (s c)"), ident16[:])
                last.then_inc(k_full, 1)

            def router(n, b):
                pe.wait_ge(zs_ready, n * KSETS + KSETS)
                if beyond(n, 1):
                    pe.wait_ge(out_ready, n - 1)
                for k in range(NC):
                    last = nc.tensor.matmul(psL[:, k * E:(k + 1) * E], ZS[:, b, k * P:(k + 1) * P], wz16[:, EC:WZ],
                                            start=True, stop=True)
                last.then_inc(l_full, 1)

            def experts(n, b, units):
                for u in units:
                    if beyond(n, 0) or u >= 2:
                        pe.wait_ge(we_ready, n * NU + (u - 1 if u >= 2 else -u))
                    for j in range(2 if u < NP else 1):
                        a = (2 * u + j) * P
                        last = nc.tensor.matmul(psE[:, u % 2, j * EC:(j + 1) * EC], ZS[:, b, a:a + P], wz16[:, 0:EC],
                                                start=True, stop=True)
                    last.then_inc(e_full, 1)

            def sums(n, c):
                for s in range(QSETS):
                    pe.wait_ge(folded, n * QSETS + s + 1)
                    if s == 0 and beyond(n, 0):
                        pe.wait_ge(out_ready, n)
                    if s == 4 and (not isinstance(n, int) or n + 1 < N):
                        pe.wait_ge(lg_ready, n + 2)
                    w = min(G, NC - G * s) * C
                    for e in range(E // 4 + 1):
                        v = (WE[:, s, e] if e < E // 4 else T1[:, c, G * s:G * s + w // C]).rearrange("p q c -> p (q c)")
                        last = nc.tensor.matmul(psB[0:w, s // 4, s % 4 * P:(s % 4 + 1) * P], v[:, 0:w], ident[:],
                                                start=(e == 0), stop=(e == E // 4))
                    last.then_inc(set_done, 1)

            def step(n, c, r):
                b = c % 2
                m, mb, mc = n - 1, 1 - b, (c - 1) % TURN
                old = beyond(n, 0)
                new = not isinstance(n, int) or n < N
                more = not isinstance(n, int) or n + 1 < N
                if more:
                    project(n + 1, mb, r + b, (0,))
                if old:
                    experts(m, mb, (2, 3, 4))
                if more:
                    project(n + 1, mb, r + b, (1,))
                if old:
                    experts(m, mb, (5, 6))
                if new:
                    pe.wait_ge(z16_ready, n + 1)
                    pe.wait_ge(z_high, n * 2 + 2)
                for s in range(KSETS):
                    if new:
                        turn_tokens(n, s)
                    if old:
                        experts(m, mb, (s + 7,))
                if new:
                    router(n, b)
                if old:
                    experts(m, mb, (11, 12))
                if new:
                    experts(n, b, (0, 1))
                if old:
                    sums(m, mc)

            pe.wait_ge(w_ready, 1)
            project(0, 0, 0, (0, 1))
            steps(pe, step)

        @block.scalar
        def _(act):
            act.wait_ge(w_zero, 1)
            load_weights(act, wz, wz0, "wz", "bz", WZ)

            def to_image(n, b, r):
                act.wait_ge(set_done, n * QSETS + QSETS)
                if beyond(n, 1):
                    act.wait_ge(out_done[b], r * STORES + FREE_OUT)
                nc.scalar.activation(OUT[:, b, 0:4 * P], psB[:, 0], ACT.Copy)
                nc.scalar.activation(OUT[:, b, 4 * P:6 * P], psB[:, 1, 0:2 * P], ACT.Copy)
                nc.scalar.activation(OUT[0:C, b, 6 * P:7 * P], psB[0:C, 1, 2 * P:3 * P], ACT.Copy).then_inc(out_ready, 1)

            def step(n, c, r):
                b = c % 2
                if not isinstance(n, int) or n < N:
                    act.wait_ge(t1_cen, n + 1)
                    nc.scalar.activation(SQ[:], XH[:], ACT.Square).then_inc(t1_sq, 1)
                    act.wait_ge(t1_var, n + 1)
                    nc.scalar.activation(lrs[:], lvar[:], ACT.Sqrt).then_inc(t1_std, 1)
                if beyond(n, 1):
                    to_image(n - 2, b, r - 1)
                if not isinstance(n, int) or n < N:
                    act.wait_ge(xh_ready, n + 1)
                    if beyond(n, 0):
                        act.wait_ge(k_full, n * KSETS)
                    for s in (0, 2):
                        nc.scalar.activation(Z16[:, :, s, :], XH[:], ACT.Copy).then_inc(z_high, 1)
                    for s in range(KSETS):
                        a = 8 * s * P
                        w = min(8 * P, TP - a)
                        act.wait_ge(k_full, n * KSETS + s + 1)
                        if s == 0 and beyond(n, 1):
                            act.wait_ge(e_full, n * NU - NU)
                        nc.scalar.activation(ZS[:, b, a:a + w], psK[:, s % 2, 0:w], ACT.Copy).then_inc(zs_ready, 1)
                    act.wait_ge(l_full, n + 1)
                    nc.scalar.activation(LG[:].rearrange("p k e -> p (k e)"), psL, ACT.Copy).then_inc(lg_ready, 1)
                    act.wait_ge(gap_ready, n + 1)
                    nc.scalar.activation(g2[:], gap[:], ACT.Exp).then_inc(gap_exp, 1)
            steps(act, step)
            to_image(N - 1, 1, (N - 1) // 2)

        @block.gpsimd
        def _(pool):
            def fold(s, h):
                w = min(G, NC - G * s)
                return nc.gpsimd.tensor_tensor(WE[:, s, 0:h, 0:w], WE[:, s, 0:h, 0:w], WE[:, s, h:2 * h, 0:w], ALU.add)

            def residual(n, c, r):
                b = c % 2
                pool.wait_ge(o_done, n * 2 + 2)
                pool.wait_ge(res_in[b], (r + 1) * 16)
                nc.gpsimd.tensor_tensor(T1[:, c], T1[:, c], RES[:, b], ALU.add).then_inc(t1_ready, 1)

            def step(n, c, r):
                b = c % 2
                if beyond(n, 0):
                    for s in range(QSETS + 1):
                        if s < QSETS:
                            pool.wait_ge(we_ready, n * NU - NU + min(2 * s + 2, NU))
                            fold(s, E // 2).then_inc(half_folded, 1)
                        if s >= 1:
                            pool.wait_ge(half_folded, n * QSETS - QSETS + s)
                            fold(s - 1, E // 4).then_inc(folded, 1)
                if not isinstance(n, int) or n + 1 < N:
                    residual(n + 1, (c + 1) % TURN, r + b)

            residual(0, 0, 0)
            steps(pool, step)

        @block.vector
        def _(dve):
            done = [0]
            base = [0]

            def mark(ins):
                done[0] += 1
                return ins.then_inc(order, 1)

            def settled():
                dve.wait_ge(order, base[0] + done[0])

            def link(ins):
                mark(ins)
                settled()

            def per_token(a, n=C):
                return a.unsqueeze(2).broadcast_to([P, a.shape[1], n])

            def weigh(n, b, units):
                if n is None:
                    return
                for u in units:
                    j = 2 if u < NP else 1
                    dve.wait_ge(e_full, n * NU + u + 1)
                    if u % 2 == 0 and beyond(n, 0):
                        dve.wait_ge(set_done, n * QSETS - QSETS + u // 2 + 1)
                    q = u % 2 * 2
                    nc.vector.tensor_tensor(WE[:, u // 2, :, q:q + j].rearrange("p e k c -> p k e c"), psE[:, u % 2, 0:j * EC].rearrange(
                        "p (k e c) -> p k e c", k=j, e=E), WT[:, b, 2 * u:2 * u + j, :].unsqueeze(3).broadcast_to(
                            [P, j, E, C]), ALU.mult).then_inc(we_ready, 1)

            def o_part(h):
                q = NP + h
                return psO[:, h, 0:q * (C + 1)].rearrange("p (k c) -> p k c", c=C + 1), rl[:, h, 0:q]

            def invert(n, h):
                o, r = o_part(h)
                dve.wait_ge(o_full, n * 2 + h + 1)
                mark(nc.vector.reciprocal(r, o[:, :, C]))

            def divide(n, c, h):
                o, r = o_part(h)
                nc.vector.tensor_tensor(T1[:, c, h * NP:h * NP + NP + h, :], o[:, :, 0:C], per_token(r),
                                        ALU.mult).then_inc(o_done, 1)

            def step(n, c, r):
                b = c % 2
                new = not isinstance(n, int) or n < N
                m, mb = (n - 1, 1 - b) if beyond(n, 0) else (None, None)
                if not new:
                    weigh(m, mb, range(NU))
                    return
                done[0] = 0
                base[0] = n * ORDER_F + start
                weigh(m, mb, (0,))
                dve.wait_ge(t1_ready, n + 1)
                mark(nc.vector.tensor_reduce(lsum[:], T1[:, c], AX.X, ALU.add))
                settled()
                mark(nc.vector.tensor_scalar(lsum[:], lsum[:], 1.0 / C, None, ALU.mult))
                weigh(m, mb, (1,))
                settled()
                nc.vector.tensor_tensor(XH[:], T1[:, c], per_token(lsum[:]), ALU.subtract).then_inc(t1_cen, 1)
                weigh(m, mb, (2,))
                dve.wait_ge(t1_sq, n + 1)
                link(nc.vector.tensor_reduce(lvar[:], SQ[:], AX.X, ALU.add))
                nc.vector.tensor_scalar(lvar[:], lvar[:], 1.0 / C, LN_EPS, ALU.mult, ALU.add).then_inc(t1_var, 1)
                weigh(m, mb, (3, 4))
                dve.wait_ge(t1_std, n + 1)
                link(nc.vector.reciprocal(lrs[:], lrs[:]))
                newton_rsqrt(link, nc.vector, lrs[:], lvar[:], ltmp[:])
                link(nc.vector.tensor_tensor(XH[:], XH[:], per_token(lrs[:]), ALU.mult))
                nc.vector.memset(XH[:, :, 0:1], 1.0).then_inc(xh_ready, 1)
                dve.wait_ge(z_high, n * 2 + 1)
                mark(nc.vector.tensor_tensor(Z16[:, :, 1, :], XH[:], Z16[:, :, 0, :], ALU.subtract))
                settled()
                nc.vector.tensor_copy(Z16[:, :, 3, :], Z16[:, :, 1, :]).then_inc(z16_ready, 1)
                weigh(m, mb, range(5, NU))
                dve.wait_ge(lg_ready, n + 1)
                rev3 = rev[:].unsqueeze(1).broadcast_to([P, NC, E])
                nxt = not isinstance(n, int) or n + 1 < N
                link(nc.vector.tensor_reduce(top1[:], LG[:], AX.X, ALU.max))
                link(nc.vector.tensor_tensor(CAND[:], LG[:], per_token(top1[:], E), ALU.is_equal))
                link(nc.vector.tensor_tensor(CAND[:], CAND[:], rev3, ALU.mult))
                link(nc.vector.tensor_reduce(cmax[:], CAND[:], AX.X, ALU.max))
                link(nc.vector.tensor_tensor(SEL1[:], CAND[:], per_token(cmax[:], E), ALU.is_equal))
                link(nc.vector.scalar_tensor_tensor(out=LG[:], in0=SEL1[:], scalar=-3e38, in1=LG[:], op0=ALU.mult,
                                                    op1=ALU.add))
                link(nc.vector.tensor_reduce(top2[:], LG[:], AX.X, ALU.max))
                nc.vector.tensor_tensor(gap[:], top2[:], top1[:], ALU.subtract).then_inc(gap_ready, 1)
                mark(nc.vector.tensor_tensor(CAND[:], LG[:], per_token(top2[:], E), ALU.is_equal))
                if nxt:
                    invert(n + 1, 0)
                settled()
                mark(nc.vector.tensor_tensor(CAND[:], CAND[:], rev3, ALU.mult))
                if nxt:
                    divide(n + 1, (c + 1) % TURN, 0)
                settled()
                mark(nc.vector.tensor_reduce(cmax[:], CAND[:], AX.X, ALU.max))
                if nxt:
                    invert(n + 1, 1)
                settled()
                mark(nc.vector.tensor_tensor(SEL2[:], CAND[:], per_token(cmax[:], E), ALU.is_equal))
                if nxt:
                    divide(n + 1, (c + 1) % TURN, 1)
                dve.wait_ge(gap_exp, n + 1)
                link(nc.vector.tensor_scalar(g1[:], g2[:], 1.0, None, ALU.add))
                link(nc.vector.reciprocal(g1[:], g1[:]))
                mark(nc.vector.tensor_tensor(g2[:], g2[:], g1[:], ALU.mult))
                mark(nc.vector.tensor_tensor(SEL1[:], SEL1[:], per_token(g1[:], E), ALU.mult))
                settled()
                link(nc.vector.tensor_tensor(SEL2[:], SEL2[:], per_token(g2[:], E), ALU.mult))
                link(nc.vector.tensor_tensor(WT[:, b], SEL1[:], SEL2[:], ALU.add))
                assert done[0] == (ORDER_F if nxt else ORDER_F - 2), done[0]

            for b, t in enumerate((wv, wv0)):
                nc.vector.memset(t[:], 0.0).then_inc(out_done[b], FREE_OUT)
            for t in (wz, wz0):
                nc.vector.memset(t[:], 0.0)
            nc.vector.memset(SUMS[:, :, T:TP], 1.0).then_inc(w_zero, 1)
            dve.wait_ge(w_zero, 1)
            dve.wait_ge(w_in, 16 * NW)
            link(nc.vector.tensor_tensor(wv[:], wv[:], wv0[:], ALU.subtract))
            link(nc.vector.tensor_tensor(wz[:], wz[:], wz0[:], ALU.subtract))
            for s in range(G):
                nc.vector.memset(wv[C * s:C * s + 1, C:C + 1], 1.0)
            link(nc.vector.tensor_copy(wz16[:], wz[:]))
            nc.vector.tensor_tensor(wz16[P // 2:P], wz[P // 2:P], wz16[P // 2:P], ALU.subtract).then_inc(w_ready, 1)
            for h in range(2):
                invert(0, h)
                settled()
                divide(0, 0, h)
            start = done[0]
            steps(dve, step)


def layouts(i):
    w8, w7 = i["L0_conv_w8"][:, 0], i["L0_conv_w7"][:, 0, 0]
    p6, p9 = i["L0_conv_p6w"][0, :, :, 0], i["L0_conv_p9w"][0, 0]
    right, left = slice(G - 1, 2 * G - 1), slice(0, G)
    return {
        "ident": np.eye(P, dtype=np.float32),
        "ident16": np.eye(P, dtype=np.float16),
        "eye4": np.tile(np.eye(C, dtype=np.float32), (G, 1)),
        "rev": np.tile(np.arange(E, 0, -1, dtype=np.float32), (P, 1)),
        "w8s": w8[:, :, 0:G].transpose(2, 0, 1).reshape(P, 5),
        "w8e": np.tile(w8[:, :, G], (G, 1)),
        "w7e": np.tile(w7, (G, 1)),
        "p6": np.stack([p6[:, right].T.reshape(P), p6[:, left].T.reshape(P)], 1),
        "p9": np.concatenate([np.repeat(p9[right], C, 0), np.repeat(p9[left], C, 0)], 1),
        "w2t": i["L0_conv_w2"][:, :, 0].transpose(2, 1, 0),
        "wqk": np.concatenate([i["L1_attn_Wq"], i["L1_attn_Wk"]], 1),
        "bqk": np.concatenate([i["L1_attn_bq"], i["L1_attn_bk"]])[None],
        "Wv": i["L1_attn_Wv"],
        "bv": i["L1_attn_bv"][None],
        "wz": np.concatenate([i["L1_ffn_expert_w"].transpose(1, 0, 2).reshape(C, E * C), i["L1_ffn_router_w"]], 1),
        "bz": np.concatenate([i["L1_ffn_expert_b"].reshape(E * C), i["L1_ffn_router_b"]])[None],
    }


def kernel(**inputs):
    import concourse.bacc as bacc
    from concourse.bass_utils import run_bass_kernel_spmd

    nc = bacc.Bacc("TRN2", target_bir_lowering=False, num_devices=1)
    inputs = {n: np.asarray(a) for n, a in inputs.items()}
    arrays = {"x": inputs["x"], **layouts(inputs)}
    arrays = {n: np.ascontiguousarray(a) for n, a in arrays.items()}
    aps = {n: nc.dram_tensor(n, a.shape, mybir.dt.from_np(a.dtype), kind="ExternalInput").ap()
           for n, a in arrays.items()}
    out = nc.dram_tensor("out", (N, C, H, W), F32, kind="ExternalOutput").ap()
    build_program(nc, aps.pop("x"), aps, out)
    r = run_bass_kernel_spmd(nc, [arrays], core_ids=[0])
    return r.results[0]["out"]
```
